# Optimizing a Trainium2 kernel written in Bass

```python
import numpy as np
import jax
import jax.numpy as jnp

def _softmax(x, axis=-1):
    return jax.nn.softmax(x, axis=axis)

def _gelu(x):
    return jax.nn.gelu(x, approximate=True)

def _silu(x):
    return jax.nn.silu(x)

def _sigmoid(x):
    return jax.nn.sigmoid(x)

def _layernorm(x, axis=-1, eps=1e-05):
    m = jnp.mean(x, axis=axis, keepdims=True)
    v = jnp.var(x, axis=axis, keepdims=True)
    return (x - m) / jnp.sqrt(v + eps)

def _scatter_add(tgt, idx, src, axis=0):
    return tgt.at[idx].add(src)

def _segment_sum(src, seg, n):
    return jax.ops.segment_sum(src, seg, n)
kernel_name = 'mk_sandwich_d1_jaxref_r8_de2e92'

def setup_inputs(seed: int=0):
    np.random.seed(seed)
    _w = jnp.asarray

    def _L0_attn_setup():
        import jax, jax.numpy as jnp
        import numpy as np
        DIM = 128
        HEADS = 16
        DIM_HEAD = 64
        SCALE = DIM_HEAD ** (-0.5)

        def _split_heads(t):
            b, n, _ = t.shape
            return t.reshape(b, n, HEADS, DIM_HEAD).transpose(0, 2, 1, 3)
        key = jax.random.key(seed)
        ks = jax.random.split(key, 7)
        init = lambda k, shape: jax.random.normal(k, shape, dtype=jnp.float32) * shape[0] ** (-0.5)
        return {'x': jax.random.normal(ks[0], (4, 512, DIM), dtype=jnp.float32), 'Wq': init(ks[1], (DIM, HEADS * DIM_HEAD)), 'Wk': init(ks[2], (DIM, HEADS * DIM_HEAD)), 'Wv': init(ks[3], (DIM, HEADS * DIM_HEAD)), 'Wg': init(ks[4], (DIM, HEADS * DIM_HEAD)), 'bg': jnp.zeros((HEADS * DIM_HEAD,), dtype=jnp.float32), 'Wo': init(ks[5], (HEADS * DIM_HEAD, DIM))}
    _L0_attn_in = _L0_attn_setup()

    def _L0_ffn_setup():
        import jax, jax.numpy as jnp
        import numpy as np
        DIM = 128

        def _reference_tuple_inner(x, W_r, W_k, W_v, mu_r, mu_k):
            B, T, C = x.shape
            x_prev = jnp.concatenate([jnp.zeros((B, 1, C), x.dtype), x[:, :-1, :]], axis=1)
            xr = mu_r * x + (1.0 - mu_r) * x_prev
            xk = mu_k * x + (1.0 - mu_k) * x_prev
            r = jax.nn.sigmoid(jnp.einsum('btc,dc->btd', xr, W_r))
            k = jnp.einsum('btc,dc->btd', xk, W_k)
            k_act = jnp.square(jax.nn.relu(k))
            out = r * jnp.einsum('btc,dc->btd', k_act, W_v)
            new_state = x[:, -1, :]
            return (out, new_state)
        key = jax.random.key(seed)
        ks = jax.random.split(key, 6)
        B, T, C = (8, 256, DIM)
        x = jax.random.normal(ks[0], (B, T, C), dtype=jnp.float32)
        s = 1.0 / np.sqrt(C)
        W_r = jax.random.uniform(ks[1], (C, C), jnp.float32, -s, s)
        W_k = jax.random.uniform(ks[2], (C, C), jnp.float32, -s, s)
        W_v = jax.random.uniform(ks[3], (C, C), jnp.float32, -s, s)
        mu_r = jax.random.uniform(ks[4], (C,), jnp.float32)
        mu_k = jax.random.uniform(ks[5], (C,), jnp.float32)
        return {'x': x, 'W_r': W_r, 'W_k': W_k, 'W_v': W_v, 'mu_r': mu_r, 'mu_k': mu_k}
    _L0_ffn_in = _L0_ffn_setup()
    _d = {'L0_attn_x': _L0_attn_in['x'], 'L0_attn_Wq': _L0_attn_in['Wq'], 'L0_attn_Wk': _L0_attn_in['Wk'], 'L0_attn_Wv': _L0_attn_in['Wv'], 'L0_attn_Wg': _L0_attn_in['Wg'], 'L0_attn_bg': _L0_attn_in['bg'], 'L0_attn_Wo': _L0_attn_in['Wo'], 'L0_ffn_W_r': _L0_ffn_in['W_r'], 'L0_ffn_W_k': _L0_ffn_in['W_k'], 'L0_ffn_W_v': _L0_ffn_in['W_v'], 'L0_ffn_mu_r': _L0_ffn_in['mu_r'], 'L0_ffn_mu_k': _L0_ffn_in['mu_k']}
    _x0 = _d['L0_attn_x']
    _d['L0_attn_x'] = jax.random.normal(jax.random.fold_in(jax.random.key(seed), 1), (8, 512, 128), dtype=_x0.dtype)
    del _x0
    return _d

def reference(L0_attn_x, L0_attn_Wq, L0_attn_Wk, L0_attn_Wv, L0_attn_Wg, L0_attn_bg, L0_attn_Wo, L0_ffn_W_r, L0_ffn_W_k, L0_ffn_W_v, L0_ffn_mu_r, L0_ffn_mu_k):

    def _L0_attn_ref(x, Wq, Wk, Wv, Wg, bg, Wo):
        import jax, jax.numpy as jnp
        import numpy as np
        DIM = 128
        HEADS = 16
        DIM_HEAD = 64
        SCALE = DIM_HEAD ** (-0.5)

        def _split_heads(t):
            b, n, _ = t.shape
            return t.reshape(b, n, HEADS, DIM_HEAD).transpose(0, 2, 1, 3)
        q = _split_heads(x @ Wq)
        k = _split_heads(x @ Wk)
        v = _split_heads(x @ Wv)
        g = _split_heads(x @ Wg + bg)
        q = jax.nn.elu(q) + 1.0
        k = jax.nn.elu(k) + 1.0
        g = jax.nn.sigmoid(g)
        kv = jnp.einsum('bhnd,bhne->bhde', k, v)
        k_sum = k.sum(axis=-2)
        z = 1.0 / jnp.clip(jnp.einsum('bhnd,bhd->bhn', q, k_sum), 1e-06)
        out = jnp.einsum('bhnd,bhde->bhne', q * SCALE, kv)
        out = out * z[..., None] * g
        b, h, n, d = out.shape
        out = out.transpose(0, 2, 1, 3).reshape(b, n, h * d)
        return out @ Wo

    def _L0_ffn_ref(x, W_r, W_k, W_v, mu_r, mu_k):
        import jax, jax.numpy as jnp
        import numpy as np
        DIM = 128

        def _reference_tuple_inner(x, W_r, W_k, W_v, mu_r, mu_k):
            B, T, C = x.shape
            x_prev = jnp.concatenate([jnp.zeros((B, 1, C), x.dtype), x[:, :-1, :]], axis=1)
            xr = mu_r * x + (1.0 - mu_r) * x_prev
            xk = mu_k * x + (1.0 - mu_k) * x_prev
            r = jax.nn.sigmoid(jnp.einsum('btc,dc->btd', xr, W_r))
            k = jnp.einsum('btc,dc->btd', xk, W_k)
            k_act = jnp.square(jax.nn.relu(k))
            out = r * jnp.einsum('btc,dc->btd', k_act, W_v)
            new_state = x[:, -1, :]
            return (out, new_state)
        return _reference_tuple_inner(x, W_r, W_k, W_v, mu_r, mu_k)[0]
    x = L0_attn_x
    x = x + _layernorm(_L0_attn_ref(_layernorm(x, axis=-1), L0_attn_Wq, L0_attn_Wk, L0_attn_Wv, L0_attn_Wg, L0_attn_bg, L0_attn_Wo), axis=-1)
    x = x + _layernorm(_L0_ffn_ref(_layernorm(x, axis=-1), L0_ffn_W_r, L0_ffn_W_k, L0_ffn_W_v, L0_ffn_mu_r, L0_ffn_mu_k), axis=-1)
    return x

_drawn_inputs = setup_inputs


def setup_inputs(seed=0):
    import zlib

    import numpy as np

    out = dict(_drawn_inputs(seed))
    spreads = {'L0_attn_bg': (0.0, 0.329)}
    factors = {}
    for name, (base, spread) in spreads.items():
        noise = np.random.default_rng([zlib.crc32(name.encode()), seed]).standard_normal(out[name].shape)
        drawn = base * np.exp(spread * noise) if base else spread * noise
        out[name] = jnp.asarray(drawn.astype(out[name].dtype))
    for name, factor in factors.items():
        out[name] = (out[name] * factor).astype(out[name].dtype)
    return out
```

```python
from contextlib import ExitStack

import numpy as np

import concourse.bass as bass
from concourse import mybir

F32 = mybir.dt.float32
F32R = mybir.dt.float32r
ACT = mybir.ActivationFunctionType
ALU = mybir.AluOpType

P = 128
B, T, C = 8, 512, 128
H, D = 16, 64
HD = H * D
NT = T // P
NC = HD // P
NK = NT * HD // T
HALF = 512
PAIRS = NC // 2
DW = 32
KVW = D + 2
YB = 4
RING = 4
A_LAG = 3
WO_LAG = 2
EPS = 1e-5
KV_SCALE = 0.5 * D ** -0.5


def constants():
    p = np.arange(P)
    ident = np.eye(P)
    sel = np.zeros((P, NC, P))
    denmask = np.zeros((P, NC, DW))
    for c in range(NC):
        for head in range(2):
            for copy in range(2):
                col = 2 * (c // 4) + head + 4 * copy
                sel[DW * (c % 4) + col, c, D * head:D * head + D] = 1.0
                denmask[D * head:D * head + D, c, col] = 1.0
    lorow = np.where((p % DW >= 4) & (p % DW < 8), -1.0, 0.0)[:, None]
    ones_row = np.where(p == C - 1, 1.0, 0.0)[:, None].repeat(2 * H, 1)
    parts = [ident, sel.reshape(P, -1), denmask.reshape(P, -1), lorow, ones_row]
    return np.ascontiguousarray(np.concatenate(parts, 1).astype(np.float32))


def sandwich(nc, x, Wq, Wk, Wv, Wg, bg, Wo, W_r, W_k, W_v, mu_r, mu_k, consts, out):
    with ExitStack() as ctx:
        def sb(name, shape, dt=F32):
            return ctx.enter_context(nc.sbuf_tensor(name, shape, dt))

        def sem(name):
            return ctx.enter_context(nc.semaphore(name))

        bank = [ctx.enter_context(nc.psum_tensor(f"bank{i}", [P, HALF], F32)) for i in range(8)]
        ybank = bank[0:YB]
        nbank = bank[4:6]
        dbank = bank[6]
        sbank = bank[7]

        cst = sb("cst", [P, P + NC * P + NC * DW + 1 + 2 * H])
        ident = cst[:, 0:P]
        sel_f = cst[:, P:P + NC * P]
        denmask = cst[:, P + NC * P:P + NC * P + NC * DW]
        lorow = cst[:, P + NC * P + NC * DW:P + NC * P + NC * DW + 1]
        ones_row = cst[:, P + NC * P + NC * DW + 1:]
        sel = sb("sel", [P, NC, P], F32R)

        w_hi = {n: sb(f"whi_{n}", [P, HD], F32R) for n in "kqgo"}
        w_lo = {n: sb(f"wlo_{n}", [P, HD], F32R) for n in "kqgo"}
        wv_aug = sb("wv_aug", [P, H, KVW])
        wm_raw = sb("wm_raw", [P, 3, C])
        wm_t = sb("wm_t", [P, 3, C])
        mu = sb("mu", [P, 2])

        x_in = sb("x_in", [P, NT, C])
        x_res = sb("x_res", [P, NT, C])
        stats0, mv0 = sb("stats0", [P, NT, 6]), sb("mv0", [P, NT, 6])
        rstd0 = sb("rstd0", [P, NT])
        xn = sb("xn", [P, NT, C])
        xn_hi, xn_lo = sb("xn_hi", [P, NT, C], F32R), sb("xn_lo", [P, NT, C], F32R)
        xt_hi, xt_lo = sb("xt_hi", [P, T], F32R), sb("xt_lo", [P, T], F32R)

        e = sb("e", [P, RING, HALF])
        k = sb("k", [P, RING, HALF])
        k_hi, k_lo = sb("k_hi", [P, RING, HALF], F32R), sb("k_lo", [P, RING, HALF], F32R)
        q = sb("q", [P, NC, T])
        th = sb("th", [P, NC, T])
        ktx = sb("ktx", [P, HD])
        kv = sb("kv", [P, NC, P])
        ksum_w = sb("ksum_w", [P, NC, DW])
        z_c, z_f = sb("z_c", [P, T]), sb("z_f", [P, T])
        z_hi, z = sb("z_hi", [P, T]), sb("z", [P, T], F32R)
        gz = sb("gz", [P, 2, T])
        o = sb("o", [P, RING, T])
        o_hi, o_lo = sb("o_hi", [P, RING, T], F32R), sb("o_lo", [P, RING, T], F32R)

        def row(tile, slots, n):
            return tile[:, slots * n:slots * n + slots, :].rearrange("p s n -> p (s n)")

        w_f = {n: row(q, HD // T, i) for i, n in enumerate("kqgv")}
        w_last = {n: row(th, HD // T, i) for i, n in enumerate("kqgv")}
        wo_f = row(o, HD // T, 0)

        attn_t = sb("attn_t", [P, T])
        stats1, mv1, rstd1 = sb("stats1", [P, NT, 6]), sb("mv1", [P, NT, 6]), sb("rstd1", [P, NT])
        stats2, mv2, rstd2 = sb("stats2", [P, NT, 6]), sb("mv2", [P, NT, 6]), sb("rstd2", [P, NT])
        stats3, mv3, rstd3 = sb("stats3", [P, NT, 6]), sb("mv3", [P, NT, 6]), sb("rstd3", [P, NT])
        nmr3 = sb("nmr3", [P, NT])
        n1, x1, x2n = sb("n1", [P, NT, C]), sb("x1", [P, NT, C]), sb("x2n", [P, NT, C])
        x2t = sb("x2t", [P, T + 1])
        dx, xr, xk = sb("dx", [P, T]), sb("xr", [P, T]), sb("xk", [P, T])
        r_t, k_relu, k_act, mix_t = sb("r_t", [P, T]), sb("k_relu", [P, T]), sb("k_act", [P, T]), sb("mix_t", [P, T])
        n3, y_out = sb("n3", [P, NT, C]), sb("y_out", [P, NT, C])
        power = sb("power", [P, NT])
        minus1 = sb("minus1", [P, 1])

        ld_w = {n: sem(f"ld_w{n}") for n in "kqgvo"}
        ld_cst, ld_mix, ld_x, ld_res, st_out = (sem(n) for n in ("ld_cst", "ld_mix", "ld_x", "ld_res", "st_out"))
        fills, w_cent, w_hi_ready, w_lo_ready = sem("fills"), sem("w_cent"), sem("w_hi_ready"), sem("w_lo_ready")
        sel_ready, wv_ready, wm_tr, wm_ready = sem("sel_ready"), sem("wv_ready"), sem("wm_tr"), sem("wm_ready")
        st0, var0, rs0, xn_ready = sem("st0"), sem("var0"), sem("rs0"), sem("xn_ready")
        xnhi_ready, xnlo_ready, xt_tr = sem("xnhi_ready"), sem("xnlo_ready"), sem("xt_tr")
        xthi_ready, xtlo_ready = sem("xthi_ready"), sem("xtlo_ready")
        yk_ready, yq_ready, yg_ready, zb_ready = sem("yk_ready"), sem("yq_ready"), sem("yg_ready"), sem("zb_ready")
        ek_ready, eq_ready, th_ready = sem("ek_ready"), sem("eq_ready"), sem("th_ready")
        k_ready, khi_ready, klo_ready, k_used = sem("k_ready"), sem("khi_ready"), sem("klo_ready"), sem("k_used")
        q_ready, ktx_ready, ktv_ready, kv_ready = sem("q_ready"), sem("ktx_ready"), sem("ktv_ready"), sem("kv_ready")
        ksum_ready, den_ready, z_step, zhi_ready = sem("ksum_ready"), sem("den_ready"), sem("z_step"), sem("zhi_ready")
        z_ready, num_ready, gz_ready, o_ready = sem("z_ready"), sem("num_ready"), sem("gz_ready"), sem("o_ready")
        ohi_ready, olo_ready, o_used, at_ready = sem("ohi_ready"), sem("olo_ready"), sem("o_used"), sem("at_ready")
        attn_tr, st1, var1, rs1, n1_ready = sem("attn_tr"), sem("st1"), sem("var1"), sem("rs1"), sem("n1_ready")
        x1_ready, st2, var2, rs2, x2n_ready = sem("x1_ready"), sem("st2"), sem("var2"), sem("rs2"), sem("x2n_ready")
        x2_tr, x2t_ready, dx_ready = sem("x2_tr"), sem("x2t_ready"), sem("dx_ready")
        xr_ready, xk_ready, mr_ready, mk_ready = sem("xr_ready"), sem("xk_ready"), sem("mr_ready"), sem("mk_ready")
        rt_ready, relu_ready, kact_ready, mv_ready = sem("rt_ready"), sem("relu_ready"), sem("kact_ready"), sem("mv_ready")
        mix_ready, mix_tr, st3, var3 = sem("mix_ready"), sem("mix_tr"), sem("st3"), sem("var3")
        rs3, nmr_ready, n3_ready, y_ready = sem("rs3"), sem("nmr_ready"), sem("n3_ready"), sem("y_ready")

        def need(eng, s, b, per, n):
            if isinstance(b, int) and b * per + n <= 0:
                return
            eng.wait_ge(s, b * per + n)

        x_v = x.rearrange("b (t p) c -> b p t c", p=P)
        out_v = out.rearrange("b (t p) c -> b p t c", p=P)
        block = ctx.enter_context(nc.Block())

        @block.sync
        def _(sp):
            def load_centred(n, w):
                sp.dma_start(w_f[n][0:112, :], w[0:112, :]).then_inc(ld_w[n], 16)
                sp.dma_start(w_f[n][112:127, :], w[112:127, :]).then_inc(ld_w[n], 16)
                last = w[C - 1:C, :]
                sp.dma_start(w_last[n][0:112, :], last.to_broadcast([112, HD])).then_inc(ld_w[n], 16)
                sp.dma_start(w_last[n][112:127, :], last.to_broadcast([15, HD])).then_inc(ld_w[n], 16)

            sp.dma_start(x_in[:, :, :], x_v[0]).then_inc(ld_x, 16)
            sp.wait_ge(fills, 1)
            load_centred("k", Wk)
            sp.dma_start(cst[:, :], consts).then_inc(ld_cst, 16)
            load_centred("q", Wq)
            load_centred("v", Wv)
            load_centred("g", Wg)
            sp.dma_start(w_f["g"][C - 1:C, :], bg.rearrange("(a n) -> a n", a=1)).then_inc(ld_w["g"], 16)
            sp.dma_start(wo_f[:, :].rearrange("p (j n) -> p j n", j=NC),
                         Wo.rearrange("(j p) n -> p j n", p=P)).then_inc(ld_w["o"], 16)
            for n, w in enumerate((W_r, W_k, W_v)):
                sp.dma_start(wm_raw[:, n, :], w).then_inc(ld_mix, 16)
            for n, m in enumerate((mu_r, mu_k)):
                sp.dma_start(mu[:, n:n + 1], m.rearrange("(c a) -> c a", a=1)).then_inc(ld_mix, 16)

            def body(b, tail, ahead):
                if ahead:
                    need(sp, xn_ready, b, NT, NT)
                    sp.dma_start(x_in[:, :, :], x_v[b + 1]).then_inc(ld_x, 16)
                need(sp, x1_ready, b, 1, 0)
                sp.dma_start(x_res[:, :, :], x_v[b]).then_inc(ld_res, 16)
                if tail:
                    need(sp, y_ready, b, 1, 0)
                    sp.dma_start(out_v[b - 1], y_out[:, :, :]).then_inc(st_out, 16)

            body(0, False, True)
            with sp.Fori(1, B - 1) as b:
                body(b, True, True)
            body(B - 1, True, False)
            sp.wait_ge(y_ready, B)
            sp.dma_start(out_v[B - 1], y_out[:, :, :]).then_inc(st_out, 16)
            sp.wait_ge(st_out, 16 * B)

        @block.tensor
        def _(pe):
            def split_matmul(dst, s_hi, s_lo, m_hi, m_lo, start=True, stop=True):
                pe.matmul(dst, s_hi, m_hi, start=start, stop=False)
                pe.matmul(dst, s_hi, m_lo, start=False, stop=False)
                return pe.matmul(dst, s_lo, m_hi, start=False, stop=stop)

            def transposes(src):
                for t in range(NT):
                    mm = pe.transpose(sbank[:, P * t:P * t + P], src(t), ident)
                return mm

            def transpose_x(b):
                need(pe, xn_ready, b, NT, NT)
                if isinstance(b, int) and b == 0:
                    pe.wait_ge(ld_cst, 16)
                transposes(lambda t: xn[:, t, :]).then_inc(xt_tr, 1)

            def project_k(b, i):
                t, half = i // 2, i % 2
                cols = slice(HALF * half, HALF * half + HALF)
                if i == 0:
                    need(pe, xthi_ready, b, 1, 1)
                    need(pe, xtlo_ready, b, 1, 1)
                if i < YB:
                    need(pe, gz_ready, b, NC, i + 1 - YB)
                else:
                    need(pe, k_ready, b, NK, i + 1 - YB)
                rows = slice(P * t, P * t + P)
                split_matmul(ybank[i % YB][:, :], xt_hi[:, rows], xt_lo[:, rows],
                             w_hi["k"][:, cols], w_lo["k"][:, cols]).then_inc(yk_ready, 1)

            def add_ktx(b, i):
                t, half = i // 2, i % 2
                if i == 0:
                    need(pe, xnhi_ready, b, 1, 1)
                    need(pe, xnlo_ready, b, 1, 1)
                if i < 2:
                    need(pe, o_ready, b, NC, i - 1)
                need(pe, khi_ready, b, NK, i + 1)
                need(pe, klo_ready, b, NK, i + 1)
                split_matmul(nbank[half][:, :], xn_hi[:, t, :], xn_lo[:, t, :],
                             k_hi[:, i % RING, :], k_lo[:, i % RING, :],
                             start=t == 0, stop=t == NT - 1).then_inc(k_used, 1)

            def ktv(b, half):
                need(pe, ktx_ready, b, 2, half + 1)
                for pair in range(PAIRS * half, PAIRS * half + PAIRS):
                    for head in range(2):
                        h = 2 * pair + head
                        at = KVW * (pair % PAIRS)
                        mm = pe.matmul(nbank[half][D * head:D * head + D, at:at + KVW],
                                       ktx[:, D * h:D * h + D], wv_aug[:, h, :], start=True, stop=True,
                                       tile_position=(0, D * head), skip_group_check=True)
                mm.then_inc(ktv_ready, 1)

            def project_q(b, c):
                if c < YB:
                    need(pe, k_ready, b, NK, c + NK + 1 - YB)
                else:
                    need(pe, q_ready, b, NC, c + 1 - YB)
                cols = slice(P * c, P * c + P)
                split_matmul(ybank[c % YB][:, :], w_hi["q"][:, cols], w_lo["q"][:, cols],
                             xt_hi[:, :], xt_lo[:, :]).then_inc(yq_ready, 1)

            def project_g(b, c):
                if c < YB:
                    need(pe, q_ready, b, NC, c + NC + 1 - YB)
                else:
                    need(pe, th_ready, b, NC, c + 1 - YB)
                cols = slice(P * c, P * c + P)
                split_matmul(ybank[c % YB][:, :], w_hi["g"][:, cols], w_lo["g"][:, cols],
                             xt_hi[:, :], xt_lo[:, :]).then_inc(yg_ready, 1)

            def denominators(b):
                need(pe, ksum_ready, b, 2, 2)
                need(pe, q_ready, b, NC, NC)
                need(pe, at_ready, b, 1, 0)
                for c in range(NC):
                    j = c % 4
                    mm = pe.matmul(dbank[DW * j:DW * j + DW, :], ksum_w[:, c, :], q[:, c, :],
                                   start=c < 4, stop=c >= 4, tile_position=(0, DW * j), skip_group_check=True)
                mm.then_inc(den_ready, 1)

            def numerator(b, c):
                if c == 0:
                    need(pe, kv_ready, b, 4, 4)
                    need(pe, ksum_ready, b, 2, 2)
                if c >= 2:
                    need(pe, o_ready, b, NC, c - 1)
                pe.matmul(nbank[c % 2][:, :], kv[:, c, :], q[:, c, :], start=True, stop=True).then_inc(num_ready, 1)

            def broadcast_z(b, c):
                if c == 0:
                    need(pe, z_ready, b, 1, 1)
                if c < YB:
                    need(pe, th_ready, b, NC, c + NC + 1 - YB)
                else:
                    need(pe, gz_ready, b, NC, c + 1 - YB)
                pe.matmul(ybank[c % YB][:, :], sel[:, c, :], z[:, :], start=True, stop=True).then_inc(zb_ready, 1)

            def project_out(b, c):
                if c == 0:
                    need(pe, z_step, b, 1, 1)
                need(pe, ohi_ready, b, NC, c + 1)
                need(pe, olo_ready, b, NC, c + 1)
                rows = slice(P * c, P * c + P)
                split_matmul(dbank[:, :], w_hi["o"][:, rows], w_lo["o"][:, rows],
                             o_hi[:, c % RING, :], o_lo[:, c % RING, :],
                             start=c == 0, stop=c == NC - 1).then_inc(o_used, 1)

            def tail_attn(b):
                need(pe, at_ready, b, 1, 1)
                need(pe, n3_ready, b, NT, 0)
                transposes(lambda t: attn_t[:, P * t:P * t + P]).then_inc(attn_tr, 1)

            def tail_x2(b):
                need(pe, x2n_ready, b, NT, NT)
                transposes(lambda t: x2n[:, t, :]).then_inc(x2_tr, 1)

            def tail_r(b):
                need(pe, xr_ready, b, 1, 1)
                pe.matmul(sbank[:, :], wm_t[:, 0, :], xr[:, :], start=True, stop=True).then_inc(mr_ready, 1)

            def tail_k(b):
                need(pe, xk_ready, b, 1, 1)
                need(pe, rt_ready, b, 1, 1)
                pe.matmul(sbank[:, :], wm_t[:, 1, :], xk[:, :], start=True, stop=True).then_inc(mk_ready, 1)

            def tail_v(b):
                need(pe, kact_ready, b, 1, 1)
                pe.matmul(sbank[:, :], wm_t[:, 2, :], k_act[:, :], start=True, stop=True).then_inc(mv_ready, 1)

            def tail_mix(b):
                need(pe, mix_ready, b, 1, 1)
                transposes(lambda t: mix_t[:, P * t:P * t + P]).then_inc(mix_tr, 1)

            def body(b, tail, ahead):
                for i in range(NK):
                    project_k(b, i)
                    if tail and i < WO_LAG:
                        project_out(b - 1, NC - WO_LAG + i)
                    if tail and i == 4:
                        tail_attn(b - 1)
                    if i >= A_LAG:
                        add_ktx(b, i - A_LAG)
                for c in range(NC):
                    project_q(b, c)
                    if c < A_LAG:
                        add_ktx(b, NK - A_LAG + c)
                    if tail and c == 3:
                        tail_x2(b - 1)
                    if c in (5, 6):
                        if c == 5:
                            pe.wait_ge(wv_ready, 2)
                        ktv(b, c - 5)
                project_g(b, 0)
                project_g(b, 1)
                if tail:
                    tail_r(b - 1)
                denominators(b)
                for c in range(2, NC):
                    project_g(b, c)
                    if tail and c == 4:
                        tail_k(b - 1)
                    if tail and c == 7:
                        tail_v(b - 1)
                numerator(b, 0)
                numerator(b, 1)
                if tail:
                    tail_mix(b - 1)
                for c in range(NC):
                    broadcast_z(b, c)
                    if c >= 2:
                        numerator(b, c)
                    if c >= WO_LAG:
                        project_out(b, c - WO_LAG)
                    if ahead and c == 3:
                        if tail:
                            need(pe, n3_ready, b, NT, 0)
                        transpose_x(b + 1)

            transpose_x(0)
            pe.wait_ge(xthi_ready, 1)
            pe.wait_ge(xtlo_ready, 1)
            pe.wait_ge(ld_mix, 80)
            for n in range(3):
                mm = pe.transpose(sbank[:, C * n:C * n + C], wm_raw[:, n, :], ident)
            mm.then_inc(wm_tr, 1)
            pe.wait_ge(w_hi_ready, 4)
            pe.wait_ge(w_lo_ready, 4)
            pe.wait_ge(sel_ready, 1)
            pe.wait_ge(wm_ready, 2)
            body(0, False, True)
            with pe.Fori(1, B - 1) as b:
                body(b, True, True)
            body(B - 1, True, False)
            for c in range(NC - WO_LAG, NC):
                project_out(B - 1, c)
            tail_attn(B - 1)
            tail_x2(B - 1)
            tail_r(B - 1)
            tail_k(B - 1)
            tail_v(B - 1)
            tail_mix(B - 1)

        @block.scalar
        def _(act):
            def split_x(b):
                need(act, xn_ready, b, NT, NT)
                need(act, k_used, b, NK, 0)
                act.activation(xn_hi[:, :, :], xn[:, :, :], ACT.Copy).then_inc(xnhi_ready, 1)

            def split_xt(b):
                need(act, xt_tr, b, 1, 1)
                need(act, yg_ready, b, NC, 0)
                act.activation(xt_hi[:, :], sbank[:, :], ACT.Copy).then_inc(xthi_ready, 1)

            def exp_k(b, i):
                need(act, yk_ready, b, NK, i + 1)
                if i < RING:
                    need(act, q_ready, b, NC, i + 1 - RING)
                else:
                    need(act, k_ready, b, NK, i + 1 - RING)
                act.activation(e[:, i % RING, :], ybank[i % YB][:, :], ACT.Exp,
                               bias=minus1[:, 0:1]).then_inc(ek_ready, 1)

            def round_k(b, i):
                need(act, k_ready, b, NK, i + 1)
                need(act, k_used, b, NK, i + 1 - RING)
                act.activation(k_hi[:, i % RING, :], k[:, i % RING, :], ACT.Copy).then_inc(khi_ready, 1)

            def exp_q(b, c):
                need(act, yq_ready, b, NC, c + 1)
                if c < RING:
                    need(act, k_ready, b, NK, c + NK + 1 - RING)
                else:
                    need(act, q_ready, b, NC, c + 1 - RING)
                act.activation(e[:, c % RING, :], ybank[c % YB][:, :], ACT.Exp,
                               bias=minus1[:, 0:1]).then_inc(eq_ready, 1)

            def tanh_g(b, c):
                need(act, yg_ready, b, NC, c + 1)
                need(act, gz_ready, b, NC, c + 1 - NC)
                act.activation(th[:, c, :], ybank[c % YB][:, :], ACT.Tanh, scale=0.5).then_inc(th_ready, 1)

            def take_ktx(b, half):
                need(act, k_used, b, NK, NK - 1 + half)
                need(act, ktv_ready, b, 2, half - 1)
                act.activation(ktx[:, HALF * half:HALF * half + HALF], nbank[half][:, :],
                               ACT.Copy).then_inc(ktx_ready, 1)

            def take_kv(b, half):
                need(act, ktv_ready, b, 2, half + 1)
                need(act, num_ready, b, NC, 0)
                pairs = slice(PAIRS * half, PAIRS * half + PAIRS)
                src = nbank[half][:, 0:PAIRS * KVW].rearrange("p (n w) -> p n w", w=KVW)
                for head in range(2):
                    d = slice(D * head, D * head + D)
                    act.activation(kv[d, pairs, d], src[d, :, 0:D], ACT.Copy, scale=KV_SCALE).then_inc(kv_ready, 1)

            def round_z(b):
                need(act, z_step, b, 2, 2)
                need(act, z_ready, b, 1, 0)
                act.activation(z_hi[:, :].bitcast(F32R), z_f[:, :], ACT.Copy).then_inc(zhi_ready, 1)

            def round_o(b, c):
                need(act, o_ready, b, NC, c + 1)
                need(act, o_used, b, NC, c + 1 - RING)
                act.activation(o_hi[:, c % RING, :], o[:, c % RING, :], ACT.Copy).then_inc(ohi_ready, 1)

            def take_attn(b):
                need(act, o_used, b, NC, NC)
                need(act, attn_tr, b, 1, 0)
                act.activation(attn_t[:, :], dbank[:, :], ACT.Copy).then_inc(at_ready, 1)

            def take_x2(b):
                need(act, x2_tr, b, 1, 1)
                need(act, xk_ready, b, 1, 0)
                act.activation(x2t[:, 1:T + 1], sbank[:, :], ACT.Copy).then_inc(x2t_ready, 1)

            def take_r(b):
                need(act, mr_ready, b, 1, 1)
                need(act, mix_ready, b, 1, 0)
                act.activation(r_t[:, :], sbank[:, :], ACT.Tanh, scale=0.5).then_inc(rt_ready, 1)

            def take_k(b):
                need(act, mk_ready, b, 1, 1)
                act.activation(k_relu[:, :], sbank[:, :], ACT.Relu).then_inc(relu_ready, 1)
                need(act, relu_ready, b, 1, 1)
                need(act, mv_ready, b, 1, 0)
                act.activation(k_act[:, :], k_relu[:, :], ACT.Square).then_inc(kact_ready, 1)

            def norm3(b):
                need(act, nmr_ready, b, 1, 1)
                need(act, y_ready, b, 1, 0)
                for t in range(NT):
                    act.activation(n3[:, t, :], sbank[:, P * t:P * t + P], ACT.Identity,
                                   bias=nmr3[:, t:t + 1], scale=rstd3[:, t:t + 1]).then_inc(n3_ready, 1)

            def round_w(n, src):
                act.activation(w_hi[n][:, :], src[:, :], ACT.Copy).then_inc(w_hi_ready, 1)

            def body(b, tail, ahead):
                if tail:
                    round_o(b - 1, NC - 1)
                for i in range(NK):
                    exp_k(b, i)
                    if i >= 1:
                        round_k(b, i - 1)
                    if tail and i == 3:
                        take_attn(b - 1)
                for c in range(NC):
                    exp_q(b, c)
                    if c == 0:
                        round_k(b, NK - 1)
                    if c == 4:
                        take_ktx(b, 0)
                        take_ktx(b, 1)
                    if tail and c == 5:
                        take_x2(b - 1)
                take_kv(b, 0)
                take_kv(b, 1)
                for c in range(NC):
                    tanh_g(b, c)
                    if tail and c == 3:
                        take_r(b - 1)
                    if tail and c == 6:
                        take_k(b - 1)
                round_z(b)
                for c in range(NC):
                    if tail and c == 2:
                        norm3(b - 1)
                    if ahead and c == 1:
                        split_x(b + 1)
                    if ahead and c == 6:
                        split_xt(b + 1)
                    if c >= 1:
                        round_o(b, c - 1)

            act.wait_ge(w_cent, 1)
            round_w("k", w_f["k"])
            split_x(0)
            split_xt(0)
            act.wait_ge(w_cent, 2)
            round_w("q", w_f["q"])
            act.wait_ge(wm_tr, 1)
            act.activation(wm_t[:, 0:2, :], sbank[:, 0:2 * C].rearrange("p (n c) -> p n c", n=2),
                           ACT.Copy).then_inc(wm_ready, 1)
            act.activation(wm_t[:, 2, :], sbank[:, 2 * C:3 * C], ACT.Copy, scale=0.5).then_inc(wm_ready, 1)
            act.wait_ge(w_cent, 3)
            round_w("g", w_f["g"])
            act.wait_ge(ld_w["o"], 16)
            round_w("o", wo_f)
            body(0, False, True)
            with act.Fori(1, B - 1) as b:
                body(b, True, True)
            body(B - 1, True, False)
            round_o(B - 1, NC - 1)
            take_attn(B - 1)
            take_x2(B - 1)
            take_r(B - 1)
            take_k(B - 1)
            norm3(B - 1)

        @block.vector
        def _(dve):
            def moments(src, stats, mv, s_st, s_var, b):
                steps = NT + 5
                for t in range(NT):
                    dve.bn_stats(stats[:, t, :], src(t)).then_inc(s_st, 1)
                need(dve, s_st, b, steps, NT)
                dve.tensor_tensor(mv[:, :, 2], stats[:, :, 1], stats[:, :, 4], ALU.subtract).then_inc(s_st, 1)
                dve.tensor_tensor(mv[:, :, 3], stats[:, :, 1], stats[:, :, 4], ALU.add).then_inc(s_st, 1)
                dve.scalar_tensor_tensor(mv[:, :, 4], stats[:, :, 2], C * EPS, stats[:, :, 5],
                                         ALU.add, ALU.add).then_inc(s_st, 1)
                need(dve, s_st, b, steps, NT + 1)
                dve.scalar_tensor_tensor(mv[:, :, 5], mv[:, :, 2], 0.25, mv[:, :, 2],
                                         ALU.mult, ALU.mult).then_inc(s_st, 1)
                need(dve, s_st, b, steps, NT + 2)
                dve.tensor_scalar(mv[:, :, 0], mv[:, :, 3], 0.5, None, ALU.mult).then_inc(s_st, 1)
                need(dve, s_st, b, steps, NT + 4)
                dve.scalar_tensor_tensor(mv[:, :, 1], mv[:, :, 4], 1.0 / C, mv[:, :, 5],
                                         ALU.mult, ALU.add).then_inc(s_var, 1)

            def moments_x(b):
                need(dve, ld_x, b, 16, 16)
                need(dve, rs0, b, 1, 0)
                need(dve, xn_ready, b, NT, 0)
                moments(lambda t: x_in[:, t, :], stats0, mv0, st0, var0, b)

            def norm_x(b):
                need(dve, rs0, b, 1, 1)
                need(dve, xt_tr, b, 1, 0)
                need(dve, xnhi_ready, b, 1, 0)
                need(dve, xnlo_ready, b, 1, 0)
                for t in range(NT):
                    dve.tensor_scalar(xn[:, t, 0:C - 1], x_in[:, t, 0:C - 1], mv0[:, t, 0:1], rstd0[:, t:t + 1],
                                      ALU.subtract, ALU.mult).then_inc(xn_ready, 1)

            def rest_xt(b):
                need(dve, xthi_ready, b, 1, 1)
                dve.tensor_tensor(xt_lo[:, :], sbank[:, :], xt_hi[:, :].bitcast(F32), ALU.subtract).then_inc(xtlo_ready, 1)

            def elu_k(b, i):
                need(dve, ek_ready, b, NK, i + 1)
                need(dve, klo_ready, b, NK, i + 1 - RING)
                dve.scalar_tensor_tensor(k[:, i % RING, :], e[:, i % RING, :], 1.0, ybank[i % YB][:, :],
                                         ALU.min, ALU.max).then_inc(k_ready, 1)

            def elu_q(b, c):
                need(dve, eq_ready, b, NC, c + 1)
                need(dve, num_ready, b, NC, c + 1 - NC)
                dve.scalar_tensor_tensor(q[:, c, :], e[:, c % RING, :], 1.0, ybank[c % YB][:, :],
                                         ALU.min, ALU.max).then_inc(q_ready, 1)

            def take_ksum(b, half):
                need(dve, kv_ready, b, 4, 2 * half + 2)
                need(dve, den_ready, b, 1, 0)
                pairs = slice(PAIRS * half, PAIRS * half + PAIRS)
                src = nbank[half][:, 0:PAIRS * KVW].rearrange("p (n w) -> p n w", w=KVW)
                dve.tensor_tensor(ksum_w[:, pairs, :], src[:, :, D:D + 1].to_broadcast([P, PAIRS, DW]),
                                  denmask[:, PAIRS * half * DW:PAIRS * (half + 1) * DW]
                                  .rearrange("p (n w) -> p n w", w=DW), ALU.mult).then_inc(ksum_ready, 1)

            def reciprocals(b):
                need(dve, den_ready, b, 1, 1)
                need(dve, z_step, b, 2, 0)
                dve.tensor_scalar(z_c[:, :], dbank[:, :], 1e-6, None, ALU.max).then_inc(z_step, 1)
                need(dve, z_step, b, 2, 1)
                need(dve, z_ready, b, 1, 0)
                dve.reciprocal(z_f[:, :], z_c[:, :]).then_inc(z_step, 1)

            def split_z(b):
                need(dve, zhi_ready, b, 1, 1)
                need(dve, zb_ready, b, NC, 0)
                dve.scalar_tensor_tensor(z[:, :], z_hi[:, :], lorow, z_f[:, :],
                                         ALU.mult, ALU.add).then_inc(z_ready, 1)

            def gate(b, c):
                need(dve, zb_ready, b, NC, c + 1)
                need(dve, th_ready, b, NC, c + 1)
                need(dve, o_ready, b, NC, c - 1)
                dve.scalar_tensor_tensor(gz[:, c % 2, :], th[:, c, :], 1.0, ybank[c % YB][:, :],
                                         ALU.add, ALU.mult).then_inc(gz_ready, 1)
                need(dve, gz_ready, b, NC, c + 1)
                need(dve, num_ready, b, NC, c + 1)
                need(dve, olo_ready, b, NC, c + 1 - RING)
                dve.tensor_tensor(o[:, c % RING, :], gz[:, c % 2, :], nbank[c % 2][:, :],
                                  ALU.mult).then_inc(o_ready, 1)

            def moments_attn(b):
                need(dve, attn_tr, b, 1, 1)
                need(dve, n1_ready, b, NT, 0)
                moments(lambda t: sbank[:, P * t:P * t + P], stats1, mv1, st1, var1, b)

            def norm_attn(b):
                need(dve, rs1, b, 1, 1)
                need(dve, x1_ready, b, 1, 0)
                for t in range(NT):
                    dve.tensor_scalar(n1[:, t, :], sbank[:, P * t:P * t + P], mv1[:, t, 0:1], rstd1[:, t:t + 1],
                                      ALU.subtract, ALU.mult).then_inc(n1_ready, 1)

            def moments_x1(b):
                need(dve, x1_ready, b, 1, 1)
                need(dve, x2n_ready, b, NT, 0)
                moments(lambda t: x1[:, t, :], stats2, mv2, st2, var2, b)

            def norm_x1(b):
                need(dve, rs2, b, 1, 1)
                need(dve, x2_tr, b, 1, 0)
                for t in range(NT):
                    dve.tensor_scalar(x2n[:, t, :], x1[:, t, :], mv2[:, t, 0:1], rstd2[:, t:t + 1],
                                      ALU.subtract, ALU.mult).then_inc(x2n_ready, 1)

            def shift(b):
                need(dve, dx_ready, b, 1, 1)
                need(dve, mr_ready, b, 1, 0)
                dve.scalar_tensor_tensor(xr[:, :], dx[:, :], mu[:, 0:1], x2t[:, 0:T],
                                         ALU.mult, ALU.add).then_inc(xr_ready, 1)
                need(dve, mk_ready, b, 1, 0)
                dve.scalar_tensor_tensor(xk[:, :], dx[:, :], mu[:, 1:2], x2t[:, 0:T],
                                         ALU.mult, ALU.add).then_inc(xk_ready, 1)

            def mix(b):
                need(dve, mv_ready, b, 1, 1)
                need(dve, rt_ready, b, 1, 1)
                need(dve, mix_tr, b, 1, 0)
                dve.scalar_tensor_tensor(mix_t[:, :], r_t[:, :], 1.0, sbank[:, :],
                                         ALU.add, ALU.mult).then_inc(mix_ready, 1)

            def moments_mix(b):
                need(dve, mix_tr, b, 1, 1)
                need(dve, n3_ready, b, NT, 0)
                moments(lambda t: sbank[:, P * t:P * t + P], stats3, mv3, st3, var3, b)

            def offsets_mix(b):
                need(dve, rs3, b, 1, 1)
                dve.scalar_tensor_tensor(nmr3[:, :], mv3[:, :, 0], -1.0, rstd3[:, :],
                                         ALU.mult, ALU.mult).then_inc(nmr_ready, 1)

            def centre(n, dst, src, last_rows, s):
                dve.tensor_tensor(dst, src, last_rows, ALU.subtract).then_inc(s, 1)

            def body(b, tail, ahead):
                for i in range(NK):
                    elu_k(b, i)
                    if tail and i == 4:
                        moments_attn(b - 1)
                    if tail and i == 6:
                        norm_attn(b - 1)
                for c in range(NC):
                    elu_q(b, c)
                    if tail and c == 0:
                        moments_x1(b - 1)
                    if tail and c == 2:
                        norm_x1(b - 1)
                    if tail and c == 7:
                        shift(b - 1)
                take_ksum(b, 0)
                take_ksum(b, 1)
                reciprocals(b)
                if ahead:
                    moments_x(b + 1)
                split_z(b)
                if tail:
                    mix(b - 1)
                if ahead:
                    norm_x(b + 1)
                for c in range(NC):
                    gate(b, c)
                    if tail and c == 0:
                        moments_mix(b - 1)
                        offsets_mix(b - 1)
                    if ahead and c == 6:
                        rest_xt(b + 1)

            dve.memset(w_f["k"][:, :], 1.0)
            dve.memset(w_last["k"][:, :], 0.0)
            dve.memset(w_f["q"][:, :], 1.0)
            dve.memset(w_f["v"][:, :], 0.0)
            dve.memset(w_last["q"][:, :], 0.0)
            dve.memset(w_last["v"][:, :], 0.0)
            dve.memset(w_last["g"][:, :], 0.0)
            dve.memset(minus1[:, :], -1.0)
            dve.memset(power[:, :], -0.5)
            dve.memset(x2t[:, 0:1], 0.0)
            dve.memset(kv[:, :, :], 0.0)
            dve.memset(xn[:, :, C - 1:C], 1.0).then_inc(fills, 1)
            moments_x(0)
            dve.wait_ge(ld_w["k"], 64)
            centre("k", w_f["k"][:, :], w_f["k"][:, :], w_last["k"][:, :], w_cent)
            norm_x(0)
            rest_xt(0)
            dve.wait_ge(ld_w["q"], 64)
            centre("q", w_f["q"][:, :], w_f["q"][:, :], w_last["q"][:, :], w_cent)
            dve.wait_ge(ld_cst, 16)
            dve.tensor_copy(sel[:, :, :], sel_f.rearrange("p (c n) -> p c n", n=P)).then_inc(sel_ready, 1)
            dve.tensor_copy(wv_aug[:, :, D:KVW], ones_row.rearrange("p (h w) -> p h w", w=2)).then_inc(wv_ready, 1)
            dve.wait_ge(ld_w["v"], 64)
            centre("v", wv_aug[:, :, 0:D], w_f["v"][:, :].rearrange("p (h d) -> p h d", d=D),
                   w_last["v"][:, :].rearrange("p (h d) -> p h d", d=D), wv_ready)
            dve.wait_ge(ld_w["g"], 80)
            centre("g", w_f["g"][:, :], w_f["g"][:, :], w_last["g"][:, :], w_cent)
            body(0, False, True)
            with dve.Fori(1, B - 1) as b:
                body(b, True, True)
            body(B - 1, True, False)
            moments_attn(B - 1)
            norm_attn(B - 1)
            moments_x1(B - 1)
            norm_x1(B - 1)
            shift(B - 1)
            mix(B - 1)
            moments_mix(B - 1)
            offsets_mix(B - 1)

        @block.gpsimd
        def _(pool):
            def rsqrt(b, var_ready, mv, rstd, s, free=None):
                need(pool, var_ready, b, 1, 1)
                pool.tensor_tensor(rstd[:, :], mv[:, :, 1], power[:, :], ALU.pow).then_inc(s, 1)

            def split_x(b):
                need(pool, xnhi_ready, b, 1, 1)
                need(pool, k_used, b, NK, 0)
                pool.tensor_tensor(xn_lo[:, :, :], xn[:, :, :], xn_hi[:, :, :].bitcast(F32), ALU.subtract).then_inc(xnlo_ready, 1)

            def rest_k(b, i):
                need(pool, khi_ready, b, NK, i + 1)
                need(pool, k_used, b, NK, i + 1 - RING)
                pool.tensor_tensor(k_lo[:, i % RING, :], k[:, i % RING, :],
                                   k_hi[:, i % RING, :].bitcast(F32), ALU.subtract).then_inc(klo_ready, 1)

            def rest_o(b, c):
                need(pool, ohi_ready, b, NC, c + 1)
                need(pool, o_used, b, NC, c + 1 - RING)
                pool.tensor_tensor(o_lo[:, c % RING, :], o[:, c % RING, :],
                                   o_hi[:, c % RING, :].bitcast(F32), ALU.subtract).then_inc(olo_ready, 1)

            def residual1(b):
                need(pool, n1_ready, b, NT, NT)
                need(pool, ld_res, b, 16, 16)
                need(pool, y_ready, b, 1, 0)
                pool.tensor_tensor(x1[:, :, :], n1[:, :, :], x_res[:, :, :], ALU.add).then_inc(x1_ready, 1)

            def difference(b):
                need(pool, x2t_ready, b, 1, 1)
                need(pool, xk_ready, b, 1, 0)
                pool.tensor_tensor(dx[:, :], x2t[:, 1:T + 1], x2t[:, 0:T], ALU.subtract).then_inc(dx_ready, 1)

            def residual2(b):
                need(pool, n3_ready, b, NT, NT)
                need(pool, st_out, b, 16, 0)
                pool.tensor_tensor(y_out[:, :, :], n3[:, :, :], x1[:, :, :], ALU.add).then_inc(y_ready, 1)

            def rest_w(n, src, count):
                pool.wait_ge(w_hi_ready, count)
                pool.tensor_tensor(w_lo[n][:, :], src[:, :], w_hi[n][:, :].bitcast(F32), ALU.subtract).then_inc(w_lo_ready, 1)

            def body(b, tail, ahead):
                if tail:
                    rest_o(b - 1, NC - 1)
                for i in range(NK):
                    rest_k(b, i)
                    if tail and i == 4:
                        rsqrt(b - 1, var1, mv1, rstd1, rs1)
                    if tail and i == 6:
                        residual1(b - 1)
                if tail:
                    rsqrt(b - 1, var2, mv2, rstd2, rs2)
                    difference(b - 1)
                if ahead:
                    rsqrt(b + 1, var0, mv0, rstd0, rs0)
                    split_x(b + 1)
                for c in range(NC - 1):
                    rest_o(b, c)
                    if tail and c == 0:
                        rsqrt(b - 1, var3, mv3, rstd3, rs3)
                    if tail and c == 3:
                        residual2(b - 1)

            pool.wait_ge(fills, 1)
            rsqrt(0, var0, mv0, rstd0, rs0)
            rest_w("k", w_f["k"], 1)
            split_x(0)
            rest_w("q", w_f["q"], 2)
            rest_w("g", w_f["g"], 3)
            rest_w("o", wo_f, 4)
            body(0, False, True)
            with pool.Fori(1, B - 1) as b:
                body(b, True, True)
            body(B - 1, True, False)
            rest_o(B - 1, NC - 1)
            rsqrt(B - 1, var1, mv1, rstd1, rs1)
            residual1(B - 1)
            rsqrt(B - 1, var2, mv2, rstd2, rs2)
            difference(B - 1)
            rsqrt(B - 1, var3, mv3, rstd3, rs3)
            residual2(B - 1)


_INS = ['L0_attn_x', 'L0_attn_Wq', 'L0_attn_Wk', 'L0_attn_Wv', 'L0_attn_Wg', 'L0_attn_bg', 'L0_attn_Wo',
        'L0_ffn_W_r', 'L0_ffn_W_k', 'L0_ffn_W_v', 'L0_ffn_mu_r', 'L0_ffn_mu_k']


def kernel(**inputs):
    import concourse.bacc as _bacc
    from concourse.bass_utils import run_bass_kernel_spmd as _run

    nc = _bacc.Bacc("TRN2", target_bir_lowering=False, num_devices=1)
    arrays = {f"in_{n}_dram": np.ascontiguousarray(inputs[n]) for n in _INS}
    arrays["in_consts_dram"] = constants()
    args = [nc.dram_tensor(n, a.shape, mybir.dt.from_np(a.dtype), kind="ExternalInput").ap()
            for n, a in arrays.items()]
    args.append(nc.dram_tensor("out_0_dram", (B, T, C), F32, kind="ExternalOutput").ap())
    sandwich(nc, *args)
    r = _run(nc, [arrays], core_ids=[0])
    return r.results[0]["out_0_dram"]
```

```python
from contextlib import ExitStack

import numpy as np

import concourse.bass as bass
from concourse import mybir

F32 = mybir.dt.float32
F32R = mybir.dt.float32r
ACT = mybir.ActivationFunctionType
ALU = mybir.AluOpType

P = 128
B, T, C = 8, 512, 128
H, D = 16, 64
HD = H * D
NT = T // P
NC = HD // P
NK = NT * HD // T
HALF = 512
PAIRS = NC // 2
DW = 32
KVW = D + 2
YB = 4
RING = 4
A_LAG = 3
WO_LAG = 2
EPS = 1e-5
KV_SCALE = 0.5 * D ** -0.5


def constants():
    p = np.arange(P)
    ident = np.eye(P)
    sel = np.zeros((P, NC, P))
    denmask = np.zeros((P, NC, DW))
    for c in range(NC):
        for head in range(2):
            for copy in range(2):
                col = 2 * (c // 4) + head + 4 * copy
                sel[DW * (c % 4) + col, c, D * head:D * head + D] = 1.0
                denmask[D * head:D * head + D, c, col] = 1.0
    ones_row = np.where(p == C - 1, 1.0, 0.0)[:, None].repeat(2 * H, 1)
    parts = [ident, sel.reshape(P, -1), denmask.reshape(P, -1), ones_row]
    return np.ascontiguousarray(np.concatenate(parts, 1).astype(np.float32))


def sandwich(nc, x, Wq, Wk, Wv, Wg, bg, Wo, W_r, W_k, W_v, mu_r, mu_k, consts, out):
    with ExitStack() as ctx:
        def sb(name, shape, dt=F32):
            return ctx.enter_context(nc.sbuf_tensor(name, shape, dt))

        def sem(name):
            return ctx.enter_context(nc.semaphore(name))

        bank = [ctx.enter_context(nc.psum_tensor(f"bank{i}", [P, HALF], F32)) for i in range(8)]
        ybank = bank[0:YB]
        kbank = bank[0:2]
        abank = bank[4:6]
        zbank = [abank[0] if c == 0 else bank[2] for c in range(NC)]
        numbank = [abank[1] if c == 0 else bank[3] for c in range(NC)]
        dbank = bank[6]
        sbank = bank[7]

        cst = sb("cst", [P, P + NC * P + NC * DW + 2 * H])
        ident = cst[:, 0:P]
        sel_f = cst[:, P:P + NC * P]
        denmask = cst[:, P + NC * P:P + NC * P + NC * DW]
        ones_row = cst[:, P + NC * P + NC * DW:]
        sel = sb("sel", [P, NC, P], F32R)

        w_hi = {n: sb(f"whi_{n}", [P, HD], F32R) for n in "kqgo"}
        w_lo = {n: sb(f"wlo_{n}", [P, HD], F32R) for n in "kqgo"}
        wv_aug = sb("wv_aug", [P, H, KVW])
        wm_raw = sb("wm_raw", [P, 3, C])
        wm_t = sb("wm_t", [P, 3, C])
        mu = sb("mu", [P, 2])

        x_in = sb("x_in", [P, NT, C])
        x_res = sb("x_res", [P, NT, C])
        stats0, mv0 = sb("stats0", [P, NT, 6]), sb("mv0", [P, NT, 6])
        rstd0 = sb("rstd0", [P, NT])
        xn = sb("xn", [P, NT, C])
        xn_hi, xn_lo = sb("xn_hi", [P, NT, C], F32R), sb("xn_lo", [P, NT, C], F32R)
        xt_hi, xt_lo = sb("xt_hi", [P, T], F32R), sb("xt_lo", [P, T], F32R)

        e = sb("e", [P, RING, HALF])
        k = q = sb("kq", [P, NC, T])
        th = o = sb("gate_out", [P, NC, T])
        k_hi, k_lo = sb("k_hi", [P, RING, HALF], F32R), sb("k_lo", [P, RING, HALF], F32R)
        o_hi, o_lo = sb("o_hi", [P, RING, T], F32R), sb("o_lo", [P, RING, T], F32R)
        ktx = sb("ktx", [P, HD])
        kv = sb("kv", [P, NC, P])
        ksum_w = sb("ksum_w", [P, NC, DW])
        den, z = sb("den", [P, T]), sb("z", [P, T], F32R)
        zt_f, zt_hi = sb("zt_f", [P, NT, 4, 4]), sb("zt_hi", [P, NT, 4, 4], F32R)
        zt = sb("zt", [P, NT, 4, DW])
        gz = sb("gz", [P, 2, T])
        tail = sb("tail", [P, 8, T])

        def rows(n):
            return tail[:, n, :].rearrange("p (t c) -> p t c", c=C)

        attn_t, dx, xr, xk, r_t = (tail[:, n, :] for n in range(5))
        n1, x1, x2n = (rows(n) for n in range(5, 8))
        w_f = {n: tail[:, 2 * i:2 * i + 2, :].rearrange("p s n -> p (s n)") for i, n in enumerate("kqgv")}
        w_last = {n: th[:, 2 * i:2 * i + 2, :].rearrange("p s n -> p (s n)") for i, n in enumerate("kqgv")}
        wo_f = gz[:, :, :].rearrange("p s n -> p (s n)")

        stats1, mv1, rstd1 = sb("stats1", [P, NT, 6]), sb("mv1", [P, NT, 6]), sb("rstd1", [P, NT])
        stats2, mv2, rstd2 = sb("stats2", [P, NT, 6]), sb("mv2", [P, NT, 6]), sb("rstd2", [P, NT])
        stats3, mv3, rstd3 = sb("stats3", [P, NT, 6]), sb("mv3", [P, NT, 6]), sb("rstd3", [P, NT])
        nmr2, nmr3 = sb("nmr2", [P, NT]), sb("nmr3", [P, NT])
        x2t = sb("x2t", [P, T + 1])
        k_relu, k_act, mix_t = sb("k_relu", [P, T]), sb("k_act", [P, T]), sb("mix_t", [P, T])
        n3, y_out = sb("n3", [P, NT, C]), sb("y_out", [P, NT, C])
        power = sb("power", [P, NT])
        minus1 = sb("minus1", [P, 1])

        ld_w = {n: sem(f"ld_w{n}") for n in "kqgvo"}
        ld_cst, ld_mix, ld_x, ld_res, st_out = (sem(n) for n in ("ld_cst", "ld_mix", "ld_x", "ld_res", "st_out"))
        fills, w_cent, w_hi_ready, w_lo_ready = sem("fills"), sem("w_cent"), sem("w_hi_ready"), sem("w_lo_ready")
        wk_ready = sem("wk_ready")
        sel_ready, wv_ready, wm_tr, wm_ready = sem("sel_ready"), sem("wv_ready"), sem("wm_tr"), sem("wm_ready")
        st0, var0, rs0, xn_ready = sem("st0"), sem("var0"), sem("rs0"), sem("xn_ready")
        xnhi_ready, xnlo_ready, xt_tr = sem("xnhi_ready"), sem("xnlo_ready"), sem("xt_tr")
        xthi_ready, xtlo_ready = sem("xthi_ready"), sem("xtlo_ready")
        yk_ready, yq_ready, yg_ready, zb_ready = sem("yk_ready"), sem("yq_ready"), sem("yg_ready"), sem("zb_ready")
        ek_ready, eq_ready, th_ready = sem("ek_ready"), sem("eq_ready"), sem("th_ready")
        k_ready, khi_ready, klo_ready, k_used = sem("k_ready"), sem("khi_ready"), sem("klo_ready"), sem("k_used")
        q_ready, ktx_ready, ktv_ready, kv_ready = sem("q_ready"), sem("ktx_ready"), sem("ktv_ready"), sem("kv_ready")
        ksum_ready, den_ready, den_out, den_tr = sem("ksum_ready"), sem("den_ready"), sem("den_out"), sem("den_tr")
        zt_step, zt_ready, z_tr = sem("zt_step"), sem("zt_ready"), sem("z_tr")
        z_ready, num_ready, gz_ready, o_ready = sem("z_ready"), sem("num_ready"), sem("gz_ready"), sem("o_ready")
        ohi_ready, olo_ready, o_used, at_ready = sem("ohi_ready"), sem("olo_ready"), sem("o_used"), sem("at_ready")
        attn_tr, st1, var1, rs1, n1_ready = sem("attn_tr"), sem("st1"), sem("var1"), sem("rs1"), sem("n1_ready")
        x1_ready, st2, var2, rs2, x2n_ready = sem("x1_ready"), sem("st2"), sem("var2"), sem("rs2"), sem("x2n_ready")
        x2_tr, x2t_ready, dx_ready = sem("x2_tr"), sem("x2t_ready"), sem("dx_ready")
        xr_ready, xk_ready, mr_ready, mk_ready = sem("xr_ready"), sem("xk_ready"), sem("mr_ready"), sem("mk_ready")
        rt_ready, relu_ready, kact_ready, mv_ready = sem("rt_ready"), sem("relu_ready"), sem("kact_ready"), sem("mv_ready")
        mix_ready, mix_tr, st3, var3 = sem("mix_ready"), sem("mix_tr"), sem("st3"), sem("var3")
        nmr2_ready = sem("nmr2_ready")
        rs3, nmr3_ready, n3_ready, y_ready = sem("rs3"), sem("nmr3_ready"), sem("n3_ready"), sem("y_ready")

        def need(eng, s, b, per, n):
            if isinstance(b, int) and b * per + n <= 0:
                return
            eng.wait_ge(s, b * per + n)

        x_v = x.rearrange("b (t p) c -> b p t c", p=P)
        out_v = out.rearrange("b (t p) c -> b p t c", p=P)
        block = ctx.enter_context(nc.Block())

        @block.sync
        def _(sp):
            def load_centred(n, w):
                sp.dma_start(w_f[n][0:112, :], w[0:112, :]).then_inc(ld_w[n], 16)
                sp.dma_start(w_f[n][112:127, :], w[112:127, :]).then_inc(ld_w[n], 16)
                last = w[C - 1:C, :]
                sp.dma_start(w_last[n][0:112, :], last.to_broadcast([112, HD])).then_inc(ld_w[n], 16)
                sp.dma_start(w_last[n][112:127, :], last.to_broadcast([15, HD])).then_inc(ld_w[n], 16)

            sp.dma_start(x_in[:, :, :], x_v[0]).then_inc(ld_x, 16)
            sp.wait_ge(fills, 1)
            load_centred("k", Wk)
            sp.dma_start(cst[:, :], consts).then_inc(ld_cst, 16)
            load_centred("q", Wq)
            load_centred("v", Wv)
            load_centred("g", Wg)
            sp.dma_start(w_f["g"][C - 1:C, :], bg.rearrange("(a n) -> a n", a=1)).then_inc(ld_w["g"], 16)
            sp.dma_start(wo_f.rearrange("p (j n) -> p j n", j=NC),
                         Wo.rearrange("(j p) n -> p j n", p=P)).then_inc(ld_w["o"], 16)
            for n, w in enumerate((W_r, W_k, W_v)):
                sp.dma_start(wm_raw[:, n, :], w).then_inc(ld_mix, 16)
            for n, m in enumerate((mu_r, mu_k)):
                sp.dma_start(mu[:, n:n + 1], m.rearrange("(c a) -> c a", a=1)).then_inc(ld_mix, 16)

            def body(b, one, two, ahead):
                if ahead:
                    need(sp, xn_ready, b, NT, NT)
                    sp.dma_start(x_in[:, :, :], x_v[b + 1]).then_inc(ld_x, 16)
                if one:
                    need(sp, x1_ready, b, 1, -1)
                    sp.dma_start(x_res[:, :, :], x_v[b - 1]).then_inc(ld_res, 16)
                if two:
                    need(sp, y_ready, b, 1, -1)
                    sp.dma_start(out_v[b - 2], y_out[:, :, :]).then_inc(st_out, 16)

            body(0, False, False, True)
            body(1, True, False, True)
            with sp.Fori(2, B - 1) as b:
                body(b, True, True, True)
            body(B - 1, True, True, False)
            body(B, True, True, False)
            sp.wait_ge(y_ready, B)
            sp.dma_start(out_v[B - 1], y_out[:, :, :]).then_inc(st_out, 16)
            sp.wait_ge(st_out, 16 * B)

        @block.tensor
        def _(pe):
            def split_matmul(dst, s_hi, s_lo, m_hi, m_lo, start=True, stop=True):
                pe.matmul(dst, s_hi, m_hi, start=start, stop=False)
                pe.matmul(dst, s_hi, m_lo, start=False, stop=False)
                return pe.matmul(dst, s_lo, m_hi, start=False, stop=stop)

            def transposes(src):
                for t in range(NT):
                    mm = pe.transpose(sbank[:, P * t:P * t + P], src(t), ident)
                return mm

            def transpose_x(b):
                need(pe, xn_ready, b, NT, NT)
                if isinstance(b, int) and b == 0:
                    pe.wait_ge(ld_cst, 16)
                transposes(lambda t: xn[:, t, :]).then_inc(xt_tr, 1)

            def project_k(b, i):
                t, half = i // 2, i % 2
                cols = slice(HALF * half, HALF * half + HALF)
                if i == 0:
                    need(pe, xthi_ready, b, 1, 1)
                    need(pe, xtlo_ready, b, 1, 1)
                if i < 2:
                    need(pe, th_ready, b, NC, i + 1 - YB)
                else:
                    need(pe, k_ready, b, NK, i - 1)
                rows = slice(P * t, P * t + P)
                split_matmul(kbank[i % 2][:, :], xt_hi[:, rows], xt_lo[:, rows],
                             w_hi["k"][:, cols], w_lo["k"][:, cols]).then_inc(yk_ready, 1)

            def add_ktx(b, i):
                t, half = i // 2, i % 2
                if i == 0:
                    need(pe, xnhi_ready, b, 1, 1)
                    need(pe, xnlo_ready, b, 1, 1)
                if i == 0:
                    need(pe, gz_ready, b, NC, 1 - NC)
                if i == 1:
                    need(pe, o_ready, b, NC, 1 - NC)
                need(pe, khi_ready, b, NK, i + 1)
                need(pe, klo_ready, b, NK, i + 1)
                split_matmul(abank[half][:, :], xn_hi[:, t, :], xn_lo[:, t, :],
                             k_hi[:, i % RING, :], k_lo[:, i % RING, :],
                             start=t == 0, stop=t == NT - 1).then_inc(k_used, 1)

            def ktv(b, half):
                need(pe, ktx_ready, b, 2, half + 1)
                for pair in range(PAIRS * half, PAIRS * half + PAIRS):
                    for head in range(2):
                        h = 2 * pair + head
                        at = KVW * (pair % PAIRS)
                        mm = pe.matmul(abank[half][D * head:D * head + D, at:at + KVW],
                                       ktx[:, D * h:D * h + D], wv_aug[:, h, :], start=True, stop=True,
                                       tile_position=(0, D * head), skip_group_check=True)
                mm.then_inc(ktv_ready, 1)

            def project_q(b, c):
                if c < 2:
                    need(pe, k_ready, b, NK, NK - 1 + c)
                elif c == 2:
                    need(pe, gz_ready, b, NC, 0)
                elif c == 3:
                    need(pe, o_ready, b, NC, 0)
                else:
                    need(pe, q_ready, b, NC, c + 1 - YB)
                cols = slice(P * c, P * c + P)
                split_matmul(ybank[c % YB][:, :], w_hi["q"][:, cols], w_lo["q"][:, cols],
                             xt_hi[:, :], xt_lo[:, :]).then_inc(yq_ready, 1)

            def project_g(b, c):
                if c < YB:
                    need(pe, q_ready, b, NC, c + NC + 1 - YB)
                else:
                    need(pe, th_ready, b, NC, c + 1 - YB)
                cols = slice(P * c, P * c + P)
                split_matmul(ybank[c % YB][:, :], w_hi["g"][:, cols], w_lo["g"][:, cols],
                             xt_hi[:, :], xt_lo[:, :]).then_inc(yg_ready, 1)

            def denominators(b, half):
                need(pe, ksum_ready, b, 2, half + 1)
                need(pe, q_ready, b, NC, 4 * half + 4)
                if half == 0:
                    need(pe, at_ready, b, 1, 0)
                for j in range(4):
                    c = 4 * half + j
                    mm = pe.matmul(dbank[DW * j:DW * j + DW, :], ksum_w[:, c, :], q[:, c, :],
                                   start=half == 0, stop=half == 1, tile_position=(0, DW * j),
                                   skip_group_check=True)
                if half == 1:
                    mm.then_inc(den_ready, 1)

            def broadcast_z(b, c):
                if c == 0:
                    need(pe, z_ready, b, 1, 1)
                    need(pe, kv_ready, b, 4, 2)
                elif c == 1:
                    need(pe, th_ready, b, NC, NC - 1)
                else:
                    need(pe, gz_ready, b, NC, c)
                pe.matmul(zbank[c][:, :], sel[:, c, :], z[:, :], start=True, stop=True).then_inc(zb_ready, 1)

            def numerator(b, c):
                if c == 0:
                    need(pe, kv_ready, b, 4, 4)
                elif c == 1:
                    need(pe, th_ready, b, NC, NC)
                else:
                    need(pe, o_ready, b, NC, c)
                pe.matmul(numbank[c][:, :], kv[:, c, :], q[:, c, :], start=True, stop=True).then_inc(num_ready, 1)

            def project_out(b, c):
                if c == 0:
                    need(pe, z_ready, b, 1, 1)
                need(pe, ohi_ready, b, NC, c + 1)
                need(pe, olo_ready, b, NC, c + 1)
                rows = slice(P * c, P * c + P)
                split_matmul(dbank[:, :], w_hi["o"][:, rows], w_lo["o"][:, rows],
                             o_hi[:, c % RING, :], o_lo[:, c % RING, :],
                             start=c == 0, stop=c == NC - 1).then_inc(o_used, 1)

            def transpose_den(b):
                need(pe, den_out, b, 1, 1)
                for t in range(NT):
                    mm = pe.transpose(dbank[:, P * t:P * t + P], den[:, P * t:P * t + P], ident)
                mm.then_inc(den_tr, 1)

            def transpose_z(b):
                need(pe, zt_ready, b, 2, 2)
                for t in range(NT):
                    mm = pe.transpose(dbank[:, P * t:P * t + P], zt[:, t, :, :], ident)
                mm.then_inc(z_tr, 1)

            def tail_attn(b):
                need(pe, at_ready, b, 1, 1)
                need(pe, n3_ready, b, NT, 0)
                transposes(lambda t: attn_t[:, P * t:P * t + P]).then_inc(attn_tr, 1)

            def tail_x2(b, after):
                need(pe, x2n_ready, b, NT, NT)
                need(pe, xthi_ready, after, 1, 1)
                need(pe, xtlo_ready, after, 1, 1)
                transposes(lambda t: x2n[:, t, :]).then_inc(x2_tr, 1)

            def tail_r(b):
                need(pe, xr_ready, b, 1, 1)
                pe.matmul(sbank[:, :], wm_t[:, 0, :], xr, start=True, stop=True).then_inc(mr_ready, 1)

            def tail_k(b):
                need(pe, xk_ready, b, 1, 1)
                need(pe, rt_ready, b, 1, 1)
                pe.matmul(sbank[:, :], wm_t[:, 1, :], xk, start=True, stop=True).then_inc(mk_ready, 1)

            def tail_v(b):
                need(pe, kact_ready, b, 1, 1)
                pe.matmul(sbank[:, :], wm_t[:, 2, :], k_act[:, :], start=True, stop=True).then_inc(mv_ready, 1)

            def tail_mix(b):
                need(pe, mix_ready, b, 1, 1)
                transposes(lambda t: mix_t[:, P * t:P * t + P]).then_inc(mix_tr, 1)

            def outputs_and_k(b, main, one, two):
                for i in range(NK):
                    for c in ((0, 1), ())[i] if i < 2 else (i,):
                        if one:
                            broadcast_z(b - 1, c)
                            numerator(b - 1, c)
                    if main:
                        project_k(b, i)
                    if main and i >= A_LAG:
                        add_ktx(b, i - A_LAG)
                    if one and i >= WO_LAG:
                        project_out(b - 1, i - WO_LAG)
                    if two and i == 1:
                        tail_x2(b - 2, b - 1 if not main else b)
                    if two and i == 4:
                        tail_r(b - 2)
                    if two and i == 5:
                        tail_k(b - 2)
                    if two and i == 6:
                        tail_v(b - 2)
                    if two and i == 7:
                        tail_mix(b - 2)

            def q_and_gate(b, one, ahead):
                first = isinstance(b, int) and b == 0
                if first:
                    pe.wait_ge(w_hi_ready, 1)
                    pe.wait_ge(w_lo_ready, 1)
                for c in range(NC):
                    project_q(b, c)
                    if c < A_LAG:
                        add_ktx(b, NK - A_LAG + c)
                    if one and c < WO_LAG:
                        project_out(b - 1, NC - WO_LAG + c)
                    if c == 4:
                        if first:
                            pe.wait_ge(wv_ready, 2)
                        ktv(b, 0)
                    if c == 5:
                        ktv(b, 1)
                    if one and c == 6:
                        tail_attn(b - 1)
                if first:
                    pe.wait_ge(w_hi_ready, 2)
                    pe.wait_ge(w_lo_ready, 2)
                project_g(b, 0)
                denominators(b, 0)
                project_g(b, 1)
                denominators(b, 1)
                for c in range(2, NC):
                    project_g(b, c)
                    if c == 3:
                        transpose_den(b)
                    if c == 6:
                        transpose_z(b)
                    if first and c == 2:
                        pe.wait_ge(ld_mix, 80)
                        for n in range(3):
                            mm = pe.transpose(sbank[:, C * n:C * n + C], wm_raw[:, n, :], ident)
                        mm.then_inc(wm_tr, 1)
                if first:
                    pe.wait_ge(wm_ready, 2)
                    pe.wait_ge(sel_ready, 1)
                    pe.wait_ge(w_hi_ready, 3)
                    pe.wait_ge(w_lo_ready, 3)
                if ahead:
                    if one:
                        need(pe, n1_ready, b, NT, 0)
                    transpose_x(b + 1)

            transpose_x(0)
            pe.wait_ge(wk_ready, 2)
            outputs_and_k(0, True, False, False)
            q_and_gate(0, False, True)
            outputs_and_k(1, True, True, False)
            q_and_gate(1, True, True)
            with pe.Fori(2, B - 1) as b:
                outputs_and_k(b, True, True, True)
                q_and_gate(b, True, True)
            outputs_and_k(B - 1, True, True, True)
            q_and_gate(B - 1, True, False)
            outputs_and_k(B, False, True, True)
            for c in range(NC - WO_LAG, NC):
                project_out(B - 1, c)
            tail_attn(B - 1)
            tail_x2(B - 1, B - 1)
            tail_r(B - 1)
            tail_k(B - 1)
            tail_v(B - 1)
            tail_mix(B - 1)

        @block.scalar
        def _(act):
            def split_x(b):
                need(act, xn_ready, b, NT, NT)
                need(act, k_used, b, NK, 0)
                act.activation(xn_hi[:, :, :], xn[:, :, :], ACT.Copy).then_inc(xnhi_ready, 1)

            def split_xt(b):
                need(act, xt_tr, b, 1, 1)
                need(act, yg_ready, b, NC, 0)
                act.activation(xt_hi[:, :], sbank[:, :], ACT.Copy).then_inc(xthi_ready, 1)

            def exp_k(b, i):
                need(act, yk_ready, b, NK, i + 1)
                if i < RING:
                    need(act, q_ready, b, NC, i + 1 - RING)
                else:
                    need(act, k_ready, b, NK, i + 1 - RING)
                act.activation(e[:, i % RING, :], kbank[i % 2][:, :], ACT.Exp,
                               bias=minus1[:, 0:1]).then_inc(ek_ready, 1)

            def round_k(b, i):
                need(act, k_ready, b, NK, i + 1)
                need(act, k_used, b, NK, i + 1 - RING)
                act.activation(k_hi[:, i % RING, :], k[:, i, :], ACT.Copy).then_inc(khi_ready, 1)

            def exp_q(b, c):
                need(act, yq_ready, b, NC, c + 1)
                if c < RING:
                    need(act, k_ready, b, NK, c + NK + 1 - RING)
                else:
                    need(act, q_ready, b, NC, c + 1 - RING)
                act.activation(e[:, c % RING, :], ybank[c % YB][:, :], ACT.Exp,
                               bias=minus1[:, 0:1]).then_inc(eq_ready, 1)

            def tanh_g(b, c):
                need(act, yg_ready, b, NC, c + 1)
                need(act, olo_ready, b, NC, c + 1 - NC)
                act.activation(th[:, c, :], ybank[c % YB][:, :], ACT.Tanh, scale=0.5).then_inc(th_ready, 1)

            def take_kv(b, half):
                need(act, ksum_ready, b, 2, half + 1)
                need(act, num_ready, b, NC, 0)
                pairs = slice(PAIRS * half, PAIRS * half + PAIRS)
                src = abank[half][:, 0:PAIRS * KVW].rearrange("p (n w) -> p n w", w=KVW)
                for head in range(2):
                    d = slice(D * head, D * head + D)
                    act.activation(kv[d, pairs, d], src[d, :, 0:D], ACT.Copy, scale=KV_SCALE).then_inc(kv_ready, 1)

            def take_z(b):
                need(act, z_tr, b, 1, 1)
                need(act, zb_ready, b, NC, 0)
                act.activation(z[:, :], dbank[:, :], ACT.Copy).then_inc(z_ready, 1)

            def round_o(b, c):
                need(act, o_ready, b, NC, c + 1)
                need(act, o_used, b, NC, c + 1 - RING)
                act.activation(o_hi[:, c % RING, :], o[:, c, :], ACT.Copy).then_inc(ohi_ready, 1)

            def take_attn(b):
                need(act, o_used, b, NC, NC)
                need(act, attn_tr, b, 1, 0)
                act.activation(attn_t, dbank[:, :], ACT.Copy).then_inc(at_ready, 1)

            def take_x2(b):
                need(act, x2_tr, b, 1, 1)
                need(act, xk_ready, b, 1, 0)
                act.activation(x2t[:, 1:T + 1], sbank[:, :], ACT.Copy).then_inc(x2t_ready, 1)

            def take_r(b):
                need(act, mr_ready, b, 1, 1)
                need(act, mix_ready, b, 1, 0)
                act.activation(r_t, sbank[:, :], ACT.Tanh, scale=0.5).then_inc(rt_ready, 1)

            def take_k(b):
                need(act, mk_ready, b, 1, 1)
                act.activation(k_relu[:, :], sbank[:, :], ACT.Relu).then_inc(relu_ready, 1)
                need(act, relu_ready, b, 1, 1)
                need(act, mv_ready, b, 1, 0)
                act.activation(k_act[:, :], k_relu[:, :], ACT.Square).then_inc(kact_ready, 1)

            def norm_x1(b):
                need(act, nmr2_ready, b, 1, 1)
                need(act, x2_tr, b, 1, 0)
                for t in range(NT):
                    act.activation(x2n[:, t, :], x1[:, t, :], ACT.Identity,
                                   bias=nmr2[:, t:t + 1], scale=rstd2[:, t:t + 1]).then_inc(x2n_ready, 1)

            def norm3(b):
                need(act, nmr3_ready, b, 1, 1)
                need(act, y_ready, b, 1, 0)
                for t in range(NT):
                    act.activation(n3[:, t, :], sbank[:, P * t:P * t + P], ACT.Identity,
                                   bias=nmr3[:, t:t + 1], scale=rstd3[:, t:t + 1]).then_inc(n3_ready, 1)

            def round_w(n, src):
                act.activation(w_hi[n][:, :], src, ACT.Copy).then_inc(w_hi_ready, 1)

            def outputs_and_k(b, main, one, two):
                for i in range(NK):
                    if two and i == 2:
                        take_x2(b - 2)
                    if two and i == 5:
                        take_r(b - 2)
                    if two and i == 6:
                        take_k(b - 2)
                    if two and i == 0:
                        norm_x1(b - 2)
                    if one and i == 0:
                        round_o(b - 1, i)
                    if main and i == 0:
                        exp_k(b, 0)
                        exp_k(b, 1)
                    if main and i > 2:
                        exp_k(b, i)
                    if one and i > 0:
                        round_o(b - 1, i)
                    if main and i == 1:
                        exp_k(b, 2)
                    if main:
                        round_k(b, i)

            def q_and_gate(b, one, two, ahead):
                first = isinstance(b, int) and b == 0
                if first:
                    act.wait_ge(w_cent, 2)
                    round_w("q", w_f["q"])
                for c in range(NC):
                    exp_q(b, c)
                    if first and c == 2:
                        act.wait_ge(w_cent, 3)
                        round_w("g", w_f["g"])
                    if two and c == 3:
                        norm3(b - 2)
                    if one and c == 2:
                        take_attn(b - 1)
                for c in range(NC):
                    tanh_g(b, c)
                    if c == 1:
                        take_kv(b, 0)
                        take_kv(b, 1)
                    if first and c == 2:
                        act.wait_ge(ld_w["o"], 16)
                        round_w("o", wo_f)
                        act.wait_ge(wm_tr, 1)
                        act.activation(wm_t[:, 0:2, :], sbank[:, 0:2 * C].rearrange("p (n c) -> p n c", n=2),
                                       ACT.Copy).then_inc(wm_ready, 1)
                        act.activation(wm_t[:, 2, :], sbank[:, 2 * C:3 * C], ACT.Copy,
                                       scale=0.5).then_inc(wm_ready, 1)
                    if c == 6:
                        take_z(b)
                if ahead:
                    split_xt(b + 1)
                    split_x(b + 1)

            split_xt(0)
            split_x(0)
            outputs_and_k(0, True, False, False)
            q_and_gate(0, False, False, True)
            outputs_and_k(1, True, True, False)
            q_and_gate(1, True, False, True)
            with act.Fori(2, B - 1) as b:
                outputs_and_k(b, True, True, True)
                q_and_gate(b, True, True, True)
            outputs_and_k(B - 1, True, True, True)
            q_and_gate(B - 1, True, True, False)
            outputs_and_k(B, False, True, True)
            norm3(B - 2)
            take_attn(B - 1)
            norm_x1(B - 1)
            take_x2(B - 1)
            take_r(B - 1)
            take_k(B - 1)
            norm3(B - 1)

        @block.vector
        def _(dve):
            def moments(src, stats, mv, s_st, s_var, b):
                steps = NT + 5
                for t in range(NT):
                    dve.bn_stats(stats[:, t, :], src(t)).then_inc(s_st, 1)
                need(dve, s_st, b, steps, NT)
                dve.tensor_tensor(mv[:, :, 2], stats[:, :, 1], stats[:, :, 4], ALU.subtract).then_inc(s_st, 1)
                dve.tensor_tensor(mv[:, :, 3], stats[:, :, 1], stats[:, :, 4], ALU.add).then_inc(s_st, 1)
                dve.scalar_tensor_tensor(mv[:, :, 4], stats[:, :, 2], C * EPS, stats[:, :, 5],
                                         ALU.add, ALU.add).then_inc(s_st, 1)
                need(dve, s_st, b, steps, NT + 1)
                dve.scalar_tensor_tensor(mv[:, :, 5], mv[:, :, 2], 0.25, mv[:, :, 2],
                                         ALU.mult, ALU.mult).then_inc(s_st, 1)
                need(dve, s_st, b, steps, NT + 2)
                dve.tensor_scalar(mv[:, :, 0], mv[:, :, 3], 0.5, None, ALU.mult).then_inc(s_st, 1)
                need(dve, s_st, b, steps, NT + 4)
                dve.scalar_tensor_tensor(mv[:, :, 1], mv[:, :, 4], 1.0 / C, mv[:, :, 5],
                                         ALU.mult, ALU.add).then_inc(s_var, 1)

            def moments_x(b):
                need(dve, ld_x, b, 16, 16)
                need(dve, rs0, b, 1, 0)
                need(dve, xn_ready, b, NT, 0)
                moments(lambda t: x_in[:, t, :], stats0, mv0, st0, var0, b)

            def norm_x(b):
                need(dve, rs0, b, 1, 1)
                need(dve, xt_tr, b, 1, 0)
                need(dve, xnhi_ready, b, 1, 0)
                need(dve, xnlo_ready, b, 1, 0)
                for t in range(NT):
                    dve.tensor_scalar(xn[:, t, 0:C - 1], x_in[:, t, 0:C - 1], mv0[:, t, 0:1], rstd0[:, t:t + 1],
                                      ALU.subtract, ALU.mult).then_inc(xn_ready, 1)

            def rest_xt(b):
                need(dve, xthi_ready, b, 1, 1)
                dve.tensor_tensor(xt_lo[:, :], sbank[:, :], xt_hi[:, :].bitcast(F32), ALU.subtract).then_inc(xtlo_ready, 1)

            def elu_k(b, i):
                need(dve, ek_ready, b, NK, i + 1)
                need(dve, num_ready, b, NC, i + 1 - NC)
                dve.scalar_tensor_tensor(k[:, i, :], e[:, i % RING, :], 1.0, kbank[i % 2][:, :],
                                         ALU.min, ALU.max).then_inc(k_ready, 1)

            def elu_q(b, c):
                need(dve, eq_ready, b, NC, c + 1)
                need(dve, klo_ready, b, NK, c + 1)
                dve.scalar_tensor_tensor(q[:, c, :], e[:, c % RING, :], 1.0, ybank[c % YB][:, :],
                                         ALU.min, ALU.max).then_inc(q_ready, 1)

            def take_ktx(b, half):
                need(dve, k_used, b, NK, NK - 1 + half)
                need(dve, ktv_ready, b, 2, half - 1)
                dve.tensor_copy(ktx[:, HALF * half:HALF * half + HALF], abank[half][:, :]).then_inc(ktx_ready, 1)

            def take_ksum(b, half):
                need(dve, ktv_ready, b, 2, half + 1)
                need(dve, den_ready, b, 1, 0)
                pairs = slice(PAIRS * half, PAIRS * half + PAIRS)
                src = abank[half][:, 0:PAIRS * KVW].rearrange("p (n w) -> p n w", w=KVW)
                dve.tensor_tensor(ksum_w[:, pairs, :], src[:, :, D:D + 1].to_broadcast([P, PAIRS, DW]),
                                  denmask[:, PAIRS * half * DW:PAIRS * (half + 1) * DW]
                                  .rearrange("p (n w) -> p n w", w=DW), ALU.mult).then_inc(ksum_ready, 1)

            def take_den(b):
                need(dve, den_ready, b, 1, 1)
                need(dve, den_tr, b, 1, 0)
                dve.tensor_scalar(den[:, :], dbank[:, :], 1e-6, None, ALU.max).then_inc(den_out, 1)

            def reciprocals(b):
                need(dve, den_tr, b, 1, 1)
                src = dbank[:, :].rearrange("p (t g w) -> p t g w", t=NT, w=DW)
                dve.reciprocal(zt_f[:, :, :, :], src[:, :, :, 0:4]).then_inc(zt_step, 1)
                need(dve, zt_step, b, 2, 1)
                need(dve, z_tr, b, 1, 0)
                dve.tensor_copy(zt_hi[:, :, :, :], zt_f[:, :, :, :]).then_inc(zt_step, 1)
                need(dve, zt_step, b, 2, 2)
                dve.tensor_copy(zt[:, :, :, 0:4], zt_hi[:, :, :, :].bitcast(F32)).then_inc(zt_ready, 1)
                dve.tensor_tensor(zt[:, :, :, 4:8], zt_f[:, :, :, :], zt_hi[:, :, :, :].bitcast(F32),
                                  ALU.subtract).then_inc(zt_ready, 1)

            def gate_z(b, c):
                need(dve, zb_ready, b, NC, c + 1)
                need(dve, th_ready, b, NC, c + 1)
                need(dve, o_ready, b, NC, c - 1)
                dve.scalar_tensor_tensor(gz[:, c % 2, :], th[:, c, :], 1.0, zbank[c][:, :],
                                         ALU.add, ALU.mult).then_inc(gz_ready, 1)

            def gate_numerator(b, c):
                need(dve, gz_ready, b, NC, c + 1)
                need(dve, num_ready, b, NC, c + 1)
                dve.tensor_tensor(o[:, c, :], gz[:, c % 2, :], numbank[c][:, :],
                                  ALU.mult).then_inc(o_ready, 1)

            def moments_attn(b):
                need(dve, attn_tr, b, 1, 1)
                need(dve, n1_ready, b, NT, 0)
                moments(lambda t: sbank[:, P * t:P * t + P], stats1, mv1, st1, var1, b)

            def norm_attn(b):
                need(dve, rs1, b, 1, 1)
                need(dve, x1_ready, b, 1, 0)
                for t in range(NT):
                    dve.tensor_scalar(n1[:, t, :], sbank[:, P * t:P * t + P], mv1[:, t, 0:1], rstd1[:, t:t + 1],
                                      ALU.subtract, ALU.mult).then_inc(n1_ready, 1)

            def moments_x1(b):
                need(dve, x1_ready, b, 1, 1)
                need(dve, x2n_ready, b, NT, 0)
                moments(lambda t: x1[:, t, :], stats2, mv2, st2, var2, b)

            def offsets_x1(b):
                need(dve, rs2, b, 1, 1)
                dve.scalar_tensor_tensor(nmr2[:, :], mv2[:, :, 0], -1.0, rstd2[:, :],
                                         ALU.mult, ALU.mult).then_inc(nmr2_ready, 1)

            def shift(b):
                need(dve, dx_ready, b, 1, 1)
                need(dve, mr_ready, b, 1, 0)
                dve.scalar_tensor_tensor(xr, dx, mu[:, 0:1], x2t[:, 0:T],
                                         ALU.mult, ALU.add).then_inc(xr_ready, 1)
                need(dve, mk_ready, b, 1, 0)
                dve.scalar_tensor_tensor(xk, dx, mu[:, 1:2], x2t[:, 0:T],
                                         ALU.mult, ALU.add).then_inc(xk_ready, 1)

            def mix(b):
                need(dve, mv_ready, b, 1, 1)
                need(dve, rt_ready, b, 1, 1)
                need(dve, mix_tr, b, 1, 0)
                dve.scalar_tensor_tensor(mix_t[:, :], r_t, 1.0, sbank[:, :],
                                         ALU.add, ALU.mult).then_inc(mix_ready, 1)

            def moments_mix(b):
                need(dve, mix_tr, b, 1, 1)
                need(dve, n3_ready, b, NT, 0)
                moments(lambda t: sbank[:, P * t:P * t + P], stats3, mv3, st3, var3, b)

            def offsets_mix(b):
                need(dve, rs3, b, 1, 1)
                dve.scalar_tensor_tensor(nmr3[:, :], mv3[:, :, 0], -1.0, rstd3[:, :],
                                         ALU.mult, ALU.mult).then_inc(nmr3_ready, 1)

            def centre(dst, src, last_rows, s):
                dve.tensor_tensor(dst, src, last_rows, ALU.subtract).then_inc(s, 1)

            def outputs_and_k(b, main, one, two, ahead):
                for i in range(NK):
                    if one and i == 0:
                        gate_z(b - 1, 0)
                    if two and i == 0:
                        offsets_x1(b - 2)
                    if main and i == 0:
                        rest_xt(b)
                    if one and i == 2:
                        gate_z(b - 1, 3)
                        gate_numerator(b - 1, 3)
                    if one and i > 3:
                        gate_z(b - 1, i)
                    if one and (i == 0 or i > 3):
                        gate_numerator(b - 1, i)
                    if one and i == 0:
                        gate_z(b - 1, 1)
                        gate_numerator(b - 1, 1)
                    if two and i == 7:
                        mix(b - 2)
                    if main:
                        elu_k(b, i)
                    if one and i == 0:
                        gate_z(b - 1, 2)
                        gate_numerator(b - 1, 2)
                    if two and i == 3:
                        shift(b - 2)

            def q_and_gate(b, one, two, ahead):
                first = isinstance(b, int) and b == 0
                if ahead:
                    moments_x(b + 1)
                for c in range(NC):
                    if first and c == 0:
                        dve.wait_ge(ld_w["q"], 64)
                        centre(w_f["q"], w_f["q"], w_last["q"], w_cent)
                        dve.wait_ge(ld_cst, 16)
                        dve.tensor_copy(wv_aug[:, :, D:KVW],
                                        ones_row.rearrange("p (h w) -> p h w", w=2)).then_inc(wv_ready, 1)
                    elu_q(b, c)
                    if c == 4:
                        take_ksum(b, 0)
                    if c == 5:
                        take_ksum(b, 1)
                    if two and c == 0:
                        moments_mix(b - 2)
                    if ahead and c == 3:
                        norm_x(b + 1)
                    if c == 1:
                        take_ktx(b, 0)
                    if c == 2:
                        take_ktx(b, 1)
                    if two and c == 2:
                        offsets_mix(b - 2)
                    if first and c == 2:
                        dve.wait_ge(ld_w["g"], 80)
                        centre(w_f["g"], w_f["g"], w_last["g"], w_cent)
                        dve.wait_ge(ld_w["v"], 64)
                        centre(wv_aug[:, :, 0:D], w_f["v"].rearrange("p (h d) -> p h d", d=D),
                               w_last["v"].rearrange("p (h d) -> p h d", d=D), wv_ready)
                if one:
                    moments_attn(b - 1)
                take_den(b)
                if one:
                    norm_attn(b - 1)
                reciprocals(b)
                if first:
                    dve.tensor_copy(sel[:, :, :], sel_f.rearrange("p (c n) -> p c n", n=P)).then_inc(sel_ready, 1)
                if one:
                    moments_x1(b - 1)

            dve.memset(w_f["k"], 1.0)
            dve.memset(w_last["k"], 0.0)
            dve.memset(w_f["q"], 1.0)
            dve.memset(w_f["v"], 0.0)
            dve.memset(w_last["q"], 0.0)
            dve.memset(w_last["v"], 0.0)
            dve.memset(w_last["g"], 0.0)
            dve.memset(minus1[:, :], -1.0)
            dve.memset(power[:, :], -0.5)
            dve.memset(x2t[:, 0:1], 0.0)
            dve.memset(kv[:, :, :], 0.0)
            dve.memset(zt[:, :, :, :], 0.0)
            dve.memset(xn[:, :, C - 1:C], 1.0).then_inc(fills, 1)
            moments_x(0)
            norm_x(0)
            dve.wait_ge(ld_w["k"], 64)
            centre(w_f["k"], w_f["k"], w_last["k"], w_cent)
            dve.wait_ge(w_cent, 1)
            dve.tensor_copy(w_hi["k"][:, :], w_f["k"]).then_inc(wk_ready, 1)
            dve.wait_ge(wk_ready, 1)
            dve.tensor_tensor(w_lo["k"][:, :], w_f["k"], w_hi["k"][:, :].bitcast(F32), ALU.subtract).then_inc(wk_ready, 1)
            outputs_and_k(0, True, False, False, True)
            q_and_gate(0, False, False, True)
            outputs_and_k(1, True, True, False, True)
            q_and_gate(1, True, False, True)
            with dve.Fori(2, B - 1) as b:
                outputs_and_k(b, True, True, True, True)
                q_and_gate(b, True, True, True)
            outputs_and_k(B - 1, True, True, True, False)
            q_and_gate(B - 1, True, True, False)
            outputs_and_k(B, False, True, True, False)
            moments_mix(B - 2)
            offsets_mix(B - 2)
            moments_attn(B - 1)
            norm_attn(B - 1)
            moments_x1(B - 1)
            offsets_x1(B - 1)
            shift(B - 1)
            mix(B - 1)
            moments_mix(B - 1)
            offsets_mix(B - 1)

        @block.gpsimd
        def _(pool):
            def rsqrt(b, var_ready, mv, rstd, s, free=None):
                need(pool, var_ready, b, 1, 1)
                pool.tensor_tensor(rstd[:, :], mv[:, :, 1], power[:, :], ALU.pow).then_inc(s, 1)

            def split_x(b):
                need(pool, xnhi_ready, b, 1, 1)
                need(pool, k_used, b, NK, 0)
                pool.tensor_tensor(xn_lo[:, :, :], xn[:, :, :], xn_hi[:, :, :].bitcast(F32), ALU.subtract).then_inc(xnlo_ready, 1)

            def rest_k(b, i):
                need(pool, khi_ready, b, NK, i + 1)
                need(pool, k_used, b, NK, i + 1 - RING)
                pool.tensor_tensor(k_lo[:, i % RING, :], k[:, i, :],
                                   k_hi[:, i % RING, :].bitcast(F32), ALU.subtract).then_inc(klo_ready, 1)

            def rest_o(b, c):
                need(pool, ohi_ready, b, NC, c + 1)
                need(pool, o_used, b, NC, c + 1 - RING)
                pool.tensor_tensor(o_lo[:, c % RING, :], o[:, c, :],
                                   o_hi[:, c % RING, :].bitcast(F32), ALU.subtract).then_inc(olo_ready, 1)

            def residual1(b):
                need(pool, n1_ready, b, NT, NT)
                need(pool, ld_res, b, 16, 16)
                need(pool, y_ready, b, 1, 0)
                pool.tensor_tensor(x1[:, :, :], n1[:, :, :], x_res[:, :, :], ALU.add).then_inc(x1_ready, 1)

            def difference(b):
                need(pool, x2t_ready, b, 1, 1)
                need(pool, xk_ready, b, 1, 0)
                pool.tensor_tensor(dx, x2t[:, 1:T + 1], x2t[:, 0:T], ALU.subtract).then_inc(dx_ready, 1)

            def residual2(b):
                need(pool, n3_ready, b, NT, NT)
                need(pool, st_out, b, 16, 0)
                pool.tensor_tensor(y_out[:, :, :], n3[:, :, :], x1[:, :, :], ALU.add).then_inc(y_ready, 1)

            def rest_w(n, src, count):
                pool.wait_ge(w_hi_ready, count)
                pool.tensor_tensor(w_lo[n][:, :], src, w_hi[n][:, :].bitcast(F32), ALU.subtract).then_inc(w_lo_ready, 1)

            def outputs_and_k(b, main, one, two, ahead):
                for i in range(NK):
                    if main and i == 0:
                        split_x(b)
                    if two and i == 2:
                        difference(b - 2)
                    if one:
                        rest_o(b - 1, i)
                    if main:
                        rest_k(b, i)

            def q_and_gate(b, one, two, ahead):
                first = isinstance(b, int) and b == 0
                if ahead:
                    rsqrt(b + 1, var0, mv0, rstd0, rs0)
                if two:
                    rsqrt(b - 2, var3, mv3, rstd3, rs3)
                if first:
                    rest_w("q", w_f["q"], 1)
                if first:
                    rest_w("g", w_f["g"], 2)
                    rest_w("o", wo_f, 3)
                if two:
                    residual2(b - 2)
                if one:
                    rsqrt(b - 1, var1, mv1, rstd1, rs1)
                    residual1(b - 1)
                    rsqrt(b - 1, var2, mv2, rstd2, rs2)

            pool.wait_ge(fills, 1)
            rsqrt(0, var0, mv0, rstd0, rs0)
            outputs_and_k(0, True, False, False, True)
            q_and_gate(0, False, False, True)
            outputs_and_k(1, True, True, False, True)
            q_and_gate(1, True, False, True)
            with pool.Fori(2, B - 1) as b:
                outputs_and_k(b, True, True, True, True)
                q_and_gate(b, True, True, True)
            outputs_and_k(B - 1, True, True, True, False)
            q_and_gate(B - 1, True, True, False)
            outputs_and_k(B, False, True, True, False)
            rsqrt(B - 2, var3, mv3, rstd3, rs3)
            residual2(B - 2)
            rsqrt(B - 1, var1, mv1, rstd1, rs1)
            residual1(B - 1)
            rsqrt(B - 1, var2, mv2, rstd2, rs2)
            difference(B - 1)
            rsqrt(B - 1, var3, mv3, rstd3, rs3)
            residual2(B - 1)


_INS = ['L0_attn_x', 'L0_attn_Wq', 'L0_attn_Wk', 'L0_attn_Wv', 'L0_attn_Wg', 'L0_attn_bg', 'L0_attn_Wo',
        'L0_ffn_W_r', 'L0_ffn_W_k', 'L0_ffn_W_v', 'L0_ffn_mu_r', 'L0_ffn_mu_k']


def kernel(**inputs):
    import concourse.bacc as _bacc
    from concourse.bass_utils import run_bass_kernel_spmd as _run

    nc = _bacc.Bacc("TRN2", target_bir_lowering=False, num_devices=1)
    arrays = {f"in_{n}_dram": np.ascontiguousarray(inputs[n]) for n in _INS}
    arrays["in_consts_dram"] = constants()
    args = [nc.dram_tensor(n, a.shape, mybir.dt.from_np(a.dtype), kind="ExternalInput").ap()
            for n, a in arrays.items()]
    args.append(nc.dram_tensor("out_0_dram", (B, T, C), F32, kind="ExternalOutput").ap())
    sandwich(nc, *args)
    r = _run(nc, [arrays], core_ids=[0])
    return r.results[0]["out_0_dram"]
```

```python
from contextlib import ExitStack

import numpy as np

import concourse.bass as bass
from concourse import mybir

F32 = mybir.dt.float32
F32R = mybir.dt.float32r
ACT = mybir.ActivationFunctionType
ALU = mybir.AluOpType

P = 128
B, T, C = 8, 512, 128
H, D = 16, 64
HD = H * D
NT = T // P
NC = HD // P
NK = NT * HD // T
HALF = 512
PAIRS = NC // 2
DW = 32
KVW = D + 2
YB = 4
RING = 4
A_LAG = 3
WO_LAG = 2
EPS = 1e-5
KV_SCALE = 0.5 * D ** -0.5


def constants():
    ident = np.eye(P)
    sel = np.zeros((P, NC, P))
    denmask = np.zeros((P, NC, DW))
    for c in range(NC):
        for head in range(2):
            for copy in range(2):
                col = 2 * (c // 4) + head + 4 * copy
                sel[DW * (c % 4) + col, c, D * head:D * head + D] = 1.0
                denmask[D * head:D * head + D, c, col] = 1.0
    ones_row = np.where(np.arange(P) == C - 1, 1.0, 0.0)[:, None].repeat(2 * H, 1)
    parts = [ident, sel.reshape(P, -1), denmask.reshape(P, -1), ones_row]
    return np.ascontiguousarray(np.concatenate(parts, 1).astype(np.float32))


def row_fill():
    return np.concatenate([np.ones((1, 2 * HD)), np.zeros((1, 5 * HD))], 1).astype(np.float32)


def sandwich(nc, x, Wq, Wk, Wv, Wg, bg, Wo, W_r, W_k, W_v, mu_r, mu_k, consts, fill, out):
    with ExitStack() as ctx:
        def sb(name, shape, dt=F32):
            return ctx.enter_context(nc.sbuf_tensor(name, shape, dt))

        def sem(name):
            return ctx.enter_context(nc.semaphore(name))

        bank = [ctx.enter_context(nc.psum_tensor(f"bank{i}", [P, HALF], F32)) for i in range(8)]
        ybank = bank[0:YB]
        abank = bank[4:6]

        def kbanks(b):
            return ybank if isinstance(b, int) and b == 0 else ybank[0:2]

        def spare(b, c):
            return c == 0 or isinstance(b, int) and b == B - 1 and c % 2 == 0

        def zbank(b, c):
            return abank[0] if spare(b, c) else bank[2]

        def numbank(b, c):
            return abank[1] if spare(b, c) else bank[3]

        dbank = bank[6]
        sbank = bank[7]

        cst = sb("cst", [P, P + NC * P + NC * DW + 2 * H])
        ident = cst[:, 0:P]
        sel_f = cst[:, P:P + NC * P]
        denmask = cst[:, P + NC * P:P + NC * P + NC * DW]
        ones_row = cst[:, P + NC * P + NC * DW:]
        sel = sb("sel", [P, NC, P], F32R)

        w_hi = {n: sb(f"whi_{n}", [P, HD], F32R) for n in "kqgo"}
        w_lo = {n: sb(f"wlo_{n}", [P, HD], F32R) for n in "kqgo"}
        wv_aug = sb("wv_aug", [P, H, KVW])
        wm_raw = sb("wm_raw", [P, 3, C])
        wm_t = sb("wm_t", [P, 3, C])
        mu = sb("mu", [P, 2])

        x_in = sb("x_in", [P, NT, C])
        x_res = sb("x_res", [P, NT, C])
        stats0, mv0 = sb("stats0", [P, NT, 6]), sb("mv0", [P, NT, 6])
        rstd0 = sb("rstd0", [P, NT])
        xn = sb("xn", [P, NT, C])
        xn_hi, xn_lo = sb("xn_hi", [P, NT, C], F32R), sb("xn_lo", [P, NT, C], F32R)
        xt_hi, xt_lo = sb("xt_hi", [P, T], F32R), sb("xt_lo", [P, T], F32R)

        e = sb("e", [P, RING, HALF])
        k = q = sb("kq", [P, NC, T])
        th = o = sb("gate_out", [P, NC, T])
        k_hi, k_lo = sb("k_hi", [P, RING, HALF], F32R), sb("k_lo", [P, RING, HALF], F32R)
        o_hi, o_lo = sb("o_hi", [P, RING, T], F32R), sb("o_lo", [P, RING, T], F32R)
        ktx = sb("ktx", [P, HD])
        kv = sb("kv", [P, NC, P])
        ksum_w = sb("ksum_w", [P, NC, DW])
        den, z = sb("den", [P, T]), sb("z", [P, T], F32R)
        zt_f, zt_hi = sb("zt_f", [P, NT, 4, 4]), sb("zt_hi", [P, NT, 4, 4], F32R)
        zt = sb("zt", [P, NT, 4, DW])
        gz = sb("gz", [P, 2, T])
        tail = sb("tail", [P, 8, T])

        def rows(n):
            return tail[:, n, :].rearrange("p (t c) -> p t c", c=C)

        attn_t, dx, xr, xk, r_t = (tail[:, n, :] for n in range(5))
        n1, x1, x2n = (rows(n) for n in range(5, 8))
        w_f = {n: tail[:, 2 * i:2 * i + 2, :].rearrange("p s n -> p (s n)") for i, n in enumerate("kqvg")}
        w_last = {n: th[:, 2 * i:2 * i + 2, :].rearrange("p s n -> p (s n)") for i, n in enumerate("kqvg")}
        wo_f = gz[:, :, :].rearrange("p s n -> p (s n)")

        last_x1 = x_in

        stats1, mv1, rstd1 = sb("stats1", [P, NT, 6]), sb("mv1", [P, NT, 6]), sb("rstd1", [P, NT])
        stats2, mv2, rstd2 = sb("stats2", [P, NT, 6]), sb("mv2", [P, NT, 6]), sb("rstd2", [P, NT])
        stats3, mv3, rstd3 = sb("stats3", [P, NT, 6]), sb("mv3", [P, NT, 6]), sb("rstd3", [P, NT])
        nmr2, nmr3 = sb("nmr2", [P, NT]), sb("nmr3", [P, NT])
        x2t = sb("x2t", [P, T + 1])
        k_relu, k_act, mix_t = sb("k_relu", [P, T]), sb("k_act", [P, T]), sb("mix_t", [P, T])
        n3, y_out = sb("n3", [P, NT, C]), sb("y_out", [P, NT, C])
        power = sb("power", [P, NT])
        minus1 = sb("minus1", [P, 1])

        ld_w = {n: sem(f"ld_w{n}") for n in "kqgvo"}
        ld_fill, ld_ident, ld_cst, ld_mix = sem("ld_fill"), sem("ld_ident"), sem("ld_cst"), sem("ld_mix")
        ld_x, ld_res, st_out = sem("ld_x"), sem("ld_res"), sem("st_out")
        fills, w_cent, w_hi_ready, w_lo_ready = sem("fills"), sem("w_cent"), sem("w_hi_ready"), sem("w_lo_ready")
        wk_hi_ready, wk_lo_ready = sem("wk_hi_ready"), sem("wk_lo_ready")
        sel_ready, wv_ready, wm_tr, wm_ready = sem("sel_ready"), sem("wv_ready"), sem("wm_tr"), sem("wm_ready")
        st0, var0, rs0, xn_ready = sem("st0"), sem("var0"), sem("rs0"), sem("xn_ready")
        xnhi_ready, xnlo_ready, xt_tr = sem("xnhi_ready"), sem("xnlo_ready"), sem("xt_tr")
        xthi_ready, xtlo_ready = sem("xthi_ready"), sem("xtlo_ready")
        yk_ready, yq_ready, yg_ready, zb_ready = sem("yk_ready"), sem("yq_ready"), sem("yg_ready"), sem("zb_ready")
        ek_ready, eq_ready, th_ready = sem("ek_ready"), sem("eq_ready"), sem("th_ready")
        k_ready, khi_ready, klo_ready, k_used = sem("k_ready"), sem("khi_ready"), sem("klo_ready"), sem("k_used")
        q_ready, ktx_ready, ktv_ready, kv_ready = sem("q_ready"), sem("ktx_ready"), sem("ktv_ready"), sem("kv_ready")
        ksum_ready, den_ready, den_out, den_tr = sem("ksum_ready"), sem("den_ready"), sem("den_out"), sem("den_tr")
        zt_step, zt_ready, z_tr = sem("zt_step"), sem("zt_ready"), sem("z_tr")
        z_ready, num_ready, gz_ready, o_ready = sem("z_ready"), sem("num_ready"), sem("gz_ready"), sem("o_ready")
        ohi_ready, olo_ready, o_used, at_ready = sem("ohi_ready"), sem("olo_ready"), sem("o_used"), sem("at_ready")
        attn_tr, st1, var1, rs1, n1_ready = sem("attn_tr"), sem("st1"), sem("var1"), sem("rs1"), sem("n1_ready")
        x1_ready, st2, var2, rs2, x2n_ready = sem("x1_ready"), sem("st2"), sem("var2"), sem("rs2"), sem("x2n_ready")
        x2_tr, x2t_ready, dx_ready = sem("x2_tr"), sem("x2t_ready"), sem("dx_ready")
        xr_ready, xk_ready, mr_ready, mk_ready = sem("xr_ready"), sem("xk_ready"), sem("mr_ready"), sem("mk_ready")
        rt_ready, relu_ready, kact_ready = sem("rt_ready"), sem("relu_ready"), sem("kact_ready")
        mv_ready, mix_ready, mix_tr, st3, var3 = sem("mv_ready"), sem("mix_ready"), sem("mix_tr"), sem("st3"), sem("var3")
        rs3, nmr2_ready, nmr3_ready = sem("rs3"), sem("nmr2_ready"), sem("nmr3_ready")
        n3_ready, y_ready = sem("n3_ready"), sem("y_ready")
        last = {n: sem(f"last_{n}") for n in (
            "attn", "attn_tr", "stats", "var", "rstd", "n1", "x1", "x2n", "x2_tr", "x2t", "dx", "xr", "xk",
            "mr", "mk", "r", "relu", "kact", "mv", "mix", "mix_tr", "offsets", "n3", "y")}

        def need(eng, s, b, per, n):
            if isinstance(b, int) and b * per + n <= 0:
                return
            eng.wait_ge(s, b * per + n)

        def tiles(h):
            return slice(NT // 2 * h, NT // 2 * (h + 1))

        def tokens(h):
            return slice(T // 2 * h, T // 2 * (h + 1))

        x_v = x.rearrange("b (t p) c -> b p t c", p=P)
        out_v = out.rearrange("b (t p) c -> b p t c", p=P)
        block = ctx.enter_context(nc.Block())

        @block.sync
        def _(sp):
            def load_centred(n, w):
                for rows in (slice(0, 112), slice(112, C - 1)):
                    last_row = w[C - 1:C, :].to_broadcast([rows.stop - rows.start, HD])
                    sp.dma_start(w_f[n][rows, :], w[rows, :]).then_inc(ld_w[n], 16)
                    sp.dma_start(w_last[n][rows, :], last_row).then_inc(ld_w[n], 16)

            sp.dma_start(x_in[:, :, :], x_v[0]).then_inc(ld_x, 16)
            load_centred("k", Wk)
            load_centred("q", Wq)
            load_centred("g", Wg)
            sp.dma_start(w_f["g"][C - 1:C, :], bg.rearrange("(a n) -> a n", a=1)).then_inc(ld_w["g"], 16)
            load_centred("v", Wv)
            sp.dma_start(wo_f.rearrange("p (j n) -> p j n", j=NC),
                         Wo.rearrange("(j p) n -> p j n", p=P)).then_inc(ld_w["o"], 16)
            for n, w in enumerate((W_r, W_k, W_v)):
                sp.dma_start(wm_raw[:, n, :], w).then_inc(ld_mix, 16)
            for n, m in enumerate((mu_r, mu_k)):
                sp.dma_start(mu[:, n:n + 1], m.rearrange("(c a) -> c a", a=1)).then_inc(ld_mix, 16)

            def body(b, one, two, ahead):
                if ahead:
                    need(sp, xn_ready, b, NT, NT)
                    sp.dma_start(x_in[:, :, :], x_v[b + 1]).then_inc(ld_x, 16)
                if one:
                    need(sp, x1_ready, b, 1, -1)
                    sp.dma_start(x_res[:, :, :], x_v[b - 1]).then_inc(ld_res, 16)
                if two:
                    need(sp, y_ready, b, 1, -1)
                    sp.dma_start(out_v[b - 2], y_out[:, :, :]).then_inc(st_out, 16)

            body(0, False, False, True)
            body(1, True, False, True)
            with sp.Fori(2, B - 1) as b:
                body(b, True, True, True)
            body(B - 1, True, True, False)
            body(B, True, True, False)
            for h in range(2):
                sp.wait_ge(last["y"], h + 1)
                sp.dma_start(out_v[B - 1][:, tiles(h), :], y_out[:, tiles(h), :]).then_inc(st_out, 16)
            sp.wait_ge(st_out, 16 * (B + 1))

        @block.tensor
        def _(pe):
            def split_matmul(dst, s_hi, s_lo, m_hi, m_lo, start=True, stop=True):
                pe.matmul(dst, s_hi, m_hi, start=start, stop=False)
                pe.matmul(dst, s_hi, m_lo, start=False, stop=False)
                return pe.matmul(dst, s_lo, m_hi, start=False, stop=stop)

            def transposes(src):
                for t in range(NT):
                    mm = pe.transpose(sbank[:, P * t:P * t + P], src(t), ident)
                return mm

            def transpose_x(b):
                need(pe, xn_ready, b, NT, NT)
                if isinstance(b, int) and b == 0:
                    pe.wait_ge(ld_ident, 16)
                transposes(lambda t: xn[:, t, :]).then_inc(xt_tr, 1)

            def project_k(b, i):
                t, half = i // 2, i % 2
                first = isinstance(b, int) and b == 0
                cols = slice(HALF * half, HALF * half + HALF)
                if i == 0:
                    need(pe, xthi_ready, b, 1, 1)
                    need(pe, xtlo_ready, b, 1, 1)
                if first and i < 2:
                    pe.wait_ge(wk_lo_ready, i + 1)
                depth = len(kbanks(b))
                if i >= depth:
                    need(pe, k_ready, b, NK, i + 1 - depth)
                elif not first:
                    need(pe, th_ready, b, NC, i + 1 - YB)
                rows = slice(P * t, P * t + P)
                split_matmul(kbanks(b)[i % len(kbanks(b))][:, :], xt_hi[:, rows], xt_lo[:, rows],
                             w_hi["k"][:, cols], w_lo["k"][:, cols]).then_inc(yk_ready, 1)

            def add_ktx(b, i):
                t, half = i // 2, i % 2
                if i == 0:
                    need(pe, xnhi_ready, b, 1, 1)
                    need(pe, xnlo_ready, b, 1, 1)
                if i == 0:
                    need(pe, gz_ready, b, NC, 1 - NC)
                if i == 1:
                    need(pe, o_ready, b, NC, 1 - NC)
                need(pe, khi_ready, b, NK, i + 1)
                need(pe, klo_ready, b, NK, i + 1)
                split_matmul(abank[half][:, :], xn_hi[:, t, :], xn_lo[:, t, :],
                             k_hi[:, i % RING, :], k_lo[:, i % RING, :],
                             start=t == 0, stop=t == NT - 1).then_inc(k_used, 1)

            def ktv(b, half):
                need(pe, ktx_ready, b, 2, half + 1)
                for pair in range(PAIRS * half, PAIRS * half + PAIRS):
                    for head in range(2):
                        h = 2 * pair + head
                        at = KVW * (pair % PAIRS)
                        mm = pe.matmul(abank[half][D * head:D * head + D, at:at + KVW],
                                       ktx[:, D * h:D * h + D], wv_aug[:, h, :], start=True, stop=True,
                                       tile_position=(0, D * head), skip_group_check=True)
                mm.then_inc(ktv_ready, 1)

            def project_q(b, c):
                if c < 2:
                    need(pe, k_ready, b, NK, NK - 1 + c)
                elif c == 2:
                    need(pe, gz_ready, b, NC, 0)
                elif c == 3:
                    need(pe, o_ready, b, NC, 0)
                else:
                    need(pe, q_ready, b, NC, c + 1 - YB)
                cols = slice(P * c, P * c + P)
                split_matmul(ybank[c % YB][:, :], w_hi["q"][:, cols], w_lo["q"][:, cols],
                             xt_hi[:, :], xt_lo[:, :]).then_inc(yq_ready, 1)

            def project_g(b, c):
                if c < YB:
                    need(pe, q_ready, b, NC, c + NC + 1 - YB)
                else:
                    need(pe, th_ready, b, NC, c + 1 - YB)
                cols = slice(P * c, P * c + P)
                split_matmul(ybank[c % YB][:, :], w_hi["g"][:, cols], w_lo["g"][:, cols],
                             xt_hi[:, :], xt_lo[:, :]).then_inc(yg_ready, 1)

            def denominators(b, half):
                need(pe, ksum_ready, b, 2, half + 1)
                need(pe, q_ready, b, NC, 4 * half + 4)
                if half == 0:
                    need(pe, at_ready, b, 1, 0)
                for j in range(4):
                    c = 4 * half + j
                    mm = pe.matmul(dbank[DW * j:DW * j + DW, :], ksum_w[:, c, :], q[:, c, :],
                                   start=half == 0, stop=half == 1, tile_position=(0, DW * j),
                                   skip_group_check=True)
                if half == 1:
                    mm.then_inc(den_ready, 1)

            def broadcast_z(b, c):
                if c == 0:
                    need(pe, z_ready, b, 1, 1)
                    need(pe, kv_ready, b, 4, 2)
                elif c == 1:
                    need(pe, th_ready, b, NC, NC - 1)
                else:
                    need(pe, gz_ready, b, NC, c - 1 if spare(b, 2) else c)
                pe.matmul(zbank(b, c)[:, :], sel[:, c, :], z[:, :], start=True, stop=True).then_inc(zb_ready, 1)

            def numerator(b, c):
                if c == 0:
                    need(pe, kv_ready, b, 4, 4)
                elif c == 1:
                    need(pe, th_ready, b, NC, NC)
                else:
                    need(pe, o_ready, b, NC, c - 1 if spare(b, 2) else c)
                pe.matmul(numbank(b, c)[:, :], kv[:, c, :], q[:, c, :], start=True, stop=True).then_inc(num_ready, 1)

            def project_out(b, c):
                if c == 0:
                    need(pe, z_ready, b, 1, 1)
                need(pe, ohi_ready, b, NC, c + 1)
                need(pe, olo_ready, b, NC, c + 1)
                rows = slice(P * c, P * c + P)
                split_matmul(dbank[:, :], w_hi["o"][:, rows], w_lo["o"][:, rows],
                             o_hi[:, c % RING, :], o_lo[:, c % RING, :],
                             start=c == 0, stop=c == NC - 1).then_inc(o_used, 1)

            def transpose_den(b):
                need(pe, den_out, b, 1, 1)
                for t in range(NT):
                    mm = pe.transpose(dbank[:, P * t:P * t + P], den[:, P * t:P * t + P], ident)
                mm.then_inc(den_tr, 1)

            def transpose_z(b):
                need(pe, zt_ready, b, 2, 2)
                for t in range(NT):
                    mm = pe.transpose(dbank[:, P * t:P * t + P], zt[:, t, :, :], ident)
                mm.then_inc(z_tr, 1)

            def tail_attn(b):
                need(pe, at_ready, b, 1, 1)
                need(pe, n3_ready, b, NT, 0)
                transposes(lambda t: attn_t[:, P * t:P * t + P]).then_inc(attn_tr, 1)

            def tail_x2(b, after):
                need(pe, x2n_ready, b, NT, NT)
                need(pe, xthi_ready, after, 1, 1)
                need(pe, xtlo_ready, after, 1, 1)
                transposes(lambda t: x2n[:, t, :]).then_inc(x2_tr, 1)

            def tail_r(b):
                need(pe, xr_ready, b, 1, 1)
                pe.matmul(sbank[:, :], wm_t[:, 0, :], xr, start=True, stop=True).then_inc(mr_ready, 1)

            def tail_k(b):
                need(pe, xk_ready, b, 1, 1)
                need(pe, rt_ready, b, 1, 1)
                pe.matmul(sbank[:, :], wm_t[:, 1, :], xk, start=True, stop=True).then_inc(mk_ready, 1)

            def tail_v(b):
                need(pe, kact_ready, b, 1, 1)
                pe.matmul(sbank[:, :], wm_t[:, 2, :], k_act[:, :], start=True, stop=True).then_inc(mv_ready, 1)

            def tail_mix(b):
                need(pe, mix_ready, b, 1, 1)
                transposes(lambda t: mix_t[:, P * t:P * t + P]).then_inc(mix_tr, 1)

            def outputs_and_k(b, main, one, two):
                for i in range(NK):
                    if one and i == 0:
                        for c in range(2):
                            broadcast_z(b - 1, c)
                            numerator(b - 1, c)
                    if one and i > 1:
                        broadcast_z(b - 1, i)
                        numerator(b - 1, i)
                    if main:
                        project_k(b, i)
                    if main and i >= A_LAG:
                        add_ktx(b, i - A_LAG)
                    if one and i >= WO_LAG:
                        project_out(b - 1, i - WO_LAG)
                    if two and i == 1:
                        tail_x2(b - 2, b if main else b - 1)
                    if two and i == 4:
                        tail_r(b - 2)
                    if two and i == 5:
                        tail_k(b - 2)
                    if two and i == 6:
                        tail_v(b - 2)
                    if not main and i == NK - 1:
                        project_out(b - 1, NC - WO_LAG)
                    if two and i == NK - 1:
                        tail_mix(b - 2)

            def q_and_gate(b, one, ahead):
                first = isinstance(b, int) and b == 0
                if first:
                    pe.wait_ge(w_hi_ready, 1)
                    pe.wait_ge(w_lo_ready, 1)
                for c in range(NC):
                    project_q(b, c)
                    if c < A_LAG:
                        add_ktx(b, NK - A_LAG + c)
                    if one and c < WO_LAG:
                        project_out(b - 1, NC - WO_LAG + c)
                    if c == 4:
                        if first:
                            pe.wait_ge(wv_ready, 2)
                        ktv(b, 0)
                    if c == 5:
                        ktv(b, 1)
                    if one and c == 6:
                        tail_attn(b - 1)
                if first:
                    pe.wait_ge(w_hi_ready, 2)
                    pe.wait_ge(w_lo_ready, 2)
                project_g(b, 0)
                denominators(b, 0)
                project_g(b, 1)
                denominators(b, 1)
                for c in range(2, NC):
                    project_g(b, c)
                    if c == 3:
                        transpose_den(b)
                    if c == 6:
                        transpose_z(b)
                    if first and c == 2:
                        pe.wait_ge(ld_mix, 80)
                        for n in range(3):
                            mm = pe.transpose(sbank[:, C * n:C * n + C], wm_raw[:, n, :], ident)
                        mm.then_inc(wm_tr, 1)
                if first:
                    pe.wait_ge(wm_ready, 2)
                    pe.wait_ge(sel_ready, 1)
                    pe.wait_ge(w_hi_ready, 3)
                    pe.wait_ge(w_lo_ready, 3)
                if ahead:
                    if one:
                        need(pe, n1_ready, b, NT, 0)
                    transpose_x(b + 1)

            transpose_x(0)
            outputs_and_k(0, True, False, False)
            q_and_gate(0, False, True)
            outputs_and_k(1, True, True, False)
            q_and_gate(1, True, True)
            with pe.Fori(2, B - 1) as b:
                outputs_and_k(b, True, True, True)
                q_and_gate(b, True, True)
            outputs_and_k(B - 1, True, True, True)
            q_and_gate(B - 1, True, False)
            outputs_and_k(B, False, True, True)
            for c in range(NC - WO_LAG + 1, NC):
                project_out(B - 1, c)

            def transposes_half(dst, src, h, s):
                for t in range(NT)[tiles(h)]:
                    mm = pe.transpose(dst[:, P * t:P * t + P], src(t), ident)
                mm.then_inc(s, 1)

            def product_half(dst, n, src, h, s):
                pe.matmul(dst[:, tokens(h)], wm_t[:, n, :], src[:, tokens(h)], start=True, stop=True).then_inc(s, 1)

            for h in range(2):
                pe.wait_ge(last["attn"], h + 1)
                transposes_half(bank[h], lambda t: attn_t[:, P * t:P * t + P], h, last["attn_tr"])
            for h in range(2):
                pe.wait_ge(last["x2n"], h + 1)
                transposes_half(bank[2 + h], lambda t: x2n[:, t, :], h, last["x2_tr"])
            for h in range(2):
                pe.wait_ge(last["xk"], h + 1)
                product_half(bank[4 + h], 1, xk, h, last["mk"])
                if h == 1:
                    pe.wait_ge(n3_ready, (B - 1) * NT)
                pe.wait_ge(last["xr"], h + 1)
                product_half(bank[6 + h], 0, xr, h, last["mr"])
            for h in range(2):
                pe.wait_ge(last["kact"], h + 1)
                product_half(bank[h], 2, k_act, h, last["mv"])
            for h in range(2):
                pe.wait_ge(last["mix"], h + 1)
                transposes_half(bank[2 + h], lambda t: mix_t[:, P * t:P * t + P], h, last["mix_tr"])

        @block.scalar
        def _(act):
            def split_x(b):
                need(act, xn_ready, b, NT, NT)
                need(act, k_used, b, NK, 0)
                act.activation(xn_hi[:, :, :], xn[:, :, :], ACT.Copy).then_inc(xnhi_ready, 1)

            def split_xt(b):
                need(act, xt_tr, b, 1, 1)
                need(act, yg_ready, b, NC, 0)
                act.activation(xt_hi[:, :], sbank[:, :], ACT.Copy).then_inc(xthi_ready, 1)

            def exp_k(b, i):
                need(act, yk_ready, b, NK, i + 1)
                if i < RING:
                    need(act, q_ready, b, NC, i + 1 - RING)
                else:
                    need(act, k_ready, b, NK, i + 1 - RING)
                act.activation(e[:, i % RING, :], kbanks(b)[i % len(kbanks(b))][:, :], ACT.Exp,
                               bias=minus1[:, 0:1]).then_inc(ek_ready, 1)

            def round_k(b, i):
                need(act, k_ready, b, NK, i + 1)
                need(act, k_used, b, NK, i + 1 - RING)
                act.activation(k_hi[:, i % RING, :], k[:, i, :], ACT.Copy).then_inc(khi_ready, 1)

            def exp_q(b, c):
                need(act, yq_ready, b, NC, c + 1)
                if c < RING:
                    need(act, k_ready, b, NK, c + NK + 1 - RING)
                else:
                    need(act, q_ready, b, NC, c + 1 - RING)
                act.activation(e[:, c % RING, :], ybank[c % YB][:, :], ACT.Exp,
                               bias=minus1[:, 0:1]).then_inc(eq_ready, 1)

            def tanh_g(b, c):
                need(act, yg_ready, b, NC, c + 1)
                need(act, olo_ready, b, NC, c + 1 - NC)
                act.activation(th[:, c, :], ybank[c % YB][:, :], ACT.Tanh, scale=0.5).then_inc(th_ready, 1)

            def take_kv(b, half):
                need(act, ksum_ready, b, 2, half + 1)
                need(act, num_ready, b, NC, 0)
                pairs = slice(PAIRS * half, PAIRS * half + PAIRS)
                src = abank[half][:, 0:PAIRS * KVW].rearrange("p (n w) -> p n w", w=KVW)
                for head in range(2):
                    d = slice(D * head, D * head + D)
                    act.activation(kv[d, pairs, d], src[d, :, 0:D], ACT.Copy, scale=KV_SCALE).then_inc(kv_ready, 1)

            def take_z(b):
                need(act, z_tr, b, 1, 1)
                need(act, zb_ready, b, NC, 0)
                act.activation(z[:, :], dbank[:, :], ACT.Copy).then_inc(z_ready, 1)

            def round_o(b, c):
                need(act, o_ready, b, NC, c + 1)
                need(act, o_used, b, NC, c + 1 - RING)
                act.activation(o_hi[:, c % RING, :], o[:, c, :], ACT.Copy).then_inc(ohi_ready, 1)

            def take_attn(b):
                need(act, o_used, b, NC, NC)
                need(act, attn_tr, b, 1, 0)
                act.activation(attn_t, dbank[:, :], ACT.Copy).then_inc(at_ready, 1)

            def take_x2(b):
                need(act, x2_tr, b, 1, 1)
                need(act, xk_ready, b, 1, 0)
                act.activation(x2t[:, 1:T + 1], sbank[:, :], ACT.Copy).then_inc(x2t_ready, 1)

            def take_r(b):
                need(act, mr_ready, b, 1, 1)
                need(act, mix_ready, b, 1, 0)
                act.activation(r_t, sbank[:, :], ACT.Tanh, scale=0.5).then_inc(rt_ready, 1)

            def take_k(b):
                need(act, mk_ready, b, 1, 1)
                act.activation(k_relu[:, :], sbank[:, :], ACT.Relu).then_inc(relu_ready, 1)
                need(act, relu_ready, b, 1, 1)
                need(act, mv_ready, b, 1, 0)
                act.activation(k_act[:, :], k_relu[:, :], ACT.Square).then_inc(kact_ready, 1)

            def norm_x1(b):
                need(act, nmr2_ready, b, 1, 1)
                need(act, x2_tr, b, 1, 0)
                for t in range(NT):
                    act.activation(x2n[:, t, :], x1[:, t, :], ACT.Identity,
                                   bias=nmr2[:, t:t + 1], scale=rstd2[:, t:t + 1]).then_inc(x2n_ready, 1)

            def norm3(b):
                need(act, nmr3_ready, b, 1, 1)
                need(act, y_ready, b, 1, 0)
                for t in range(NT):
                    act.activation(n3[:, t, :], sbank[:, P * t:P * t + P], ACT.Identity,
                                   bias=nmr3[:, t:t + 1], scale=rstd3[:, t:t + 1]).then_inc(n3_ready, 1)

            def round_w(n, src):
                act.activation(w_hi[n][:, :], src, ACT.Copy).then_inc(w_hi_ready, 1)

            def outputs_and_k(b, main, one, two):
                first = isinstance(b, int) and b == 0
                for i in range(NK):
                    if i == 0:
                        if two:
                            norm_x1(b - 2)
                        if one:
                            round_o(b - 1, 0)
                        if main:
                            exp_k(b, 0)
                            exp_k(b, 1)
                    if two and i == 2:
                        take_x2(b - 2)
                    if two and i == 5:
                        take_r(b - 2)
                    if two and i == 6:
                        take_k(b - 2)
                    if main and i > 2 and not first:
                        exp_k(b, i)
                    if one and i > 0:
                        round_o(b - 1, i)
                    if main and i == 1 or first and 1 < i < NK - 1:
                        exp_k(b, i + 1)
                    if first and i == 2:
                        act.wait_ge(w_cent, 3)
                        round_w("q", w_f["q"])
                    if first and i == 4:
                        act.wait_ge(w_cent, 4)
                        round_w("g", w_f["g"])
                    if first and i == 6:
                        act.wait_ge(ld_w["o"], 16)
                        round_w("o", wo_f)
                    if main:
                        round_k(b, i)

            def q_and_gate(b, one, two, ahead):
                first = isinstance(b, int) and b == 0
                for c in range(NC):
                    exp_q(b, c)
                    if two and c == 3:
                        norm3(b - 2)
                    if one and c == 2:
                        take_attn(b - 1)
                for c in range(NC):
                    tanh_g(b, c)
                    if c == 1:
                        take_kv(b, 0)
                        take_kv(b, 1)
                    if first and c == 2:
                        act.wait_ge(wm_tr, 1)
                        act.activation(wm_t[:, 0:2, :], sbank[:, 0:2 * C].rearrange("p (n c) -> p n c", n=2),
                                       ACT.Copy).then_inc(wm_ready, 1)
                        act.activation(wm_t[:, 2, :], sbank[:, 2 * C:3 * C], ACT.Copy,
                                       scale=0.5).then_inc(wm_ready, 1)
                    if c == 6:
                        take_z(b)
                if ahead:
                    split_xt(b + 1)
                    split_x(b + 1)

            act.dma_start(ident, consts[:, 0:P]).then_inc(ld_ident, 16)
            act.dma_start(tail[C - 1:C, 0:6, :].rearrange("p s n -> p (s n)"),
                         fill[0:1, 0:3 * HD]).then_inc(ld_fill, 16)
            act.dma_start(th[C - 1:C, :, :].rearrange("p s n -> p (s n)"),
                         fill[0:1, 3 * HD:]).then_inc(ld_fill, 16)
            act.dma_start(cst[:, P:], consts[:, P:]).then_inc(ld_cst, 16)
            act.wait_ge(fills, 1)
            act.activation(nmr3[:, 0:1], minus1[:, 0:1], ACT.Exp)
            split_xt(0)
            for half in range(2):
                cols = slice(HALF * half, HALF * half + HALF)
                act.wait_ge(w_cent, half + 1)
                act.activation(w_hi["k"][:, cols], w_f["k"][:, cols], ACT.Copy).then_inc(wk_hi_ready, 1)
            split_x(0)
            outputs_and_k(0, True, False, False)
            q_and_gate(0, False, False, True)
            outputs_and_k(1, True, True, False)
            q_and_gate(1, True, False, True)
            with act.Fori(2, B - 1) as b:
                outputs_and_k(b, True, True, True)
                q_and_gate(b, True, True, True)
            outputs_and_k(B - 1, True, True, True)
            q_and_gate(B - 1, True, True, False)
            outputs_and_k(B, False, True, True)

            act.wait_ge(o_used, B * NC)
            act.wait_ge(attn_tr, B - 1)
            for h in range(2):
                act.activation(attn_t[:, tokens(h)], dbank[:, tokens(h)], ACT.Copy).then_inc(last["attn"], 1)
            norm3(B - 2)
            act.wait_ge(xk_ready, B - 1)
            for h in range(2):
                act.wait_ge(last["x2_tr"], h + 1)
                act.activation(x2t[:, T // 2 * h + 1:T // 2 * (h + 1) + 1], bank[2 + h][:, tokens(h)],
                               ACT.Copy).then_inc(last["x2t"], 1)
            act.wait_ge(mix_ready, B - 1)
            for h in range(2):
                act.wait_ge(last["mk"], h + 1)
                act.activation(k_relu[:, tokens(h)], bank[4 + h][:, tokens(h)], ACT.Relu).then_inc(last["relu"], 1)
                act.wait_ge(last["mr"], h + 1)
                act.activation(r_t[:, tokens(h)], bank[6 + h][:, tokens(h)], ACT.Tanh, scale=0.5).then_inc(last["r"], 1)
            act.wait_ge(y_ready, B - 1)
            for h in range(2):
                act.wait_ge(last["offsets"], h + 1)
                for t in range(NT)[tiles(h)]:
                    act.activation(n3[:, t, :], bank[2 + h][:, P * t:P * t + P], ACT.Identity,
                                   bias=nmr3[:, t:t + 1], scale=rstd3[:, t:t + 1]).then_inc(last["n3"], 1)

        @block.vector
        def _(dve):
            def moments(src, stats, mv, s_st, s_var, b, n=slice(0, NT)):
                count = n.stop - n.start
                steps = count + 5
                for t in range(n.start, n.stop):
                    dve.bn_stats(stats[:, t, :], src(t)).then_inc(s_st, 1)
                need(dve, s_st, b, steps, count)
                dve.tensor_tensor(mv[:, n, 2], stats[:, n, 1], stats[:, n, 4], ALU.subtract).then_inc(s_st, 1)
                dve.tensor_tensor(mv[:, n, 3], stats[:, n, 1], stats[:, n, 4], ALU.add).then_inc(s_st, 1)
                dve.scalar_tensor_tensor(mv[:, n, 4], stats[:, n, 2], C * EPS, stats[:, n, 5],
                                         ALU.add, ALU.add).then_inc(s_st, 1)
                need(dve, s_st, b, steps, count + 1)
                dve.scalar_tensor_tensor(mv[:, n, 5], mv[:, n, 2], 0.25, mv[:, n, 2],
                                         ALU.mult, ALU.mult).then_inc(s_st, 1)
                need(dve, s_st, b, steps, count + 2)
                dve.tensor_scalar(mv[:, n, 0], mv[:, n, 3], 0.5, None, ALU.mult).then_inc(s_st, 1)
                need(dve, s_st, b, steps, count + 4)
                dve.scalar_tensor_tensor(mv[:, n, 1], mv[:, n, 4], 1.0 / C, mv[:, n, 5],
                                         ALU.mult, ALU.add).then_inc(s_var, 1)

            def moments_x(b):
                need(dve, ld_x, b, 16, 16)
                need(dve, rs0, b, 1, 0)
                need(dve, xn_ready, b, NT, 0)
                moments(lambda t: x_in[:, t, :], stats0, mv0, st0, var0, b)

            def norm_x(b):
                need(dve, rs0, b, 1, 1)
                need(dve, xt_tr, b, 1, 0)
                need(dve, xnhi_ready, b, 1, 0)
                need(dve, xnlo_ready, b, 1, 0)
                for t in range(NT):
                    dve.tensor_scalar(xn[:, t, 0:C - 1], x_in[:, t, 0:C - 1], mv0[:, t, 0:1], rstd0[:, t:t + 1],
                                      ALU.subtract, ALU.mult).then_inc(xn_ready, 1)

            def rest_xt(b):
                need(dve, xthi_ready, b, 1, 1)
                dve.tensor_tensor(xt_lo[:, :], sbank[:, :], xt_hi[:, :].bitcast(F32),
                                  ALU.subtract).then_inc(xtlo_ready, 1)

            def elu_k(b, i):
                need(dve, ek_ready, b, NK, i + 1)
                need(dve, num_ready, b, NC, i + 1 - NC)
                dve.scalar_tensor_tensor(k[:, i, :], e[:, i % RING, :], 1.0, kbanks(b)[i % len(kbanks(b))][:, :],
                                         ALU.min, ALU.max).then_inc(k_ready, 1)

            def elu_q(b, c):
                need(dve, eq_ready, b, NC, c + 1)
                need(dve, klo_ready, b, NK, c + 1)
                dve.scalar_tensor_tensor(q[:, c, :], e[:, c % RING, :], 1.0, ybank[c % YB][:, :],
                                         ALU.min, ALU.max).then_inc(q_ready, 1)

            def take_ktx(b, half):
                need(dve, k_used, b, NK, NK - 1 + half)
                need(dve, ktv_ready, b, 2, half - 1)
                dve.tensor_copy(ktx[:, HALF * half:HALF * half + HALF], abank[half][:, :]).then_inc(ktx_ready, 1)

            def take_ksum(b, half):
                need(dve, ktv_ready, b, 2, half + 1)
                need(dve, den_ready, b, 1, 0)
                pairs = slice(PAIRS * half, PAIRS * half + PAIRS)
                src = abank[half][:, 0:PAIRS * KVW].rearrange("p (n w) -> p n w", w=KVW)
                dve.tensor_tensor(ksum_w[:, pairs, :], src[:, :, D:D + 1].to_broadcast([P, PAIRS, DW]),
                                  denmask[:, PAIRS * half * DW:PAIRS * (half + 1) * DW]
                                  .rearrange("p (n w) -> p n w", w=DW), ALU.mult).then_inc(ksum_ready, 1)

            def take_den(b):
                need(dve, den_ready, b, 1, 1)
                need(dve, den_tr, b, 1, 0)
                dve.tensor_scalar(den[:, :], dbank[:, :], 1e-6, None, ALU.max).then_inc(den_out, 1)

            def reciprocals(b):
                need(dve, den_tr, b, 1, 1)
                src = dbank[:, :].rearrange("p (t g w) -> p t g w", t=NT, w=DW)
                dve.reciprocal(zt_f[:, :, :, :], src[:, :, :, 0:4]).then_inc(zt_step, 1)
                need(dve, zt_step, b, 2, 1)
                need(dve, z_tr, b, 1, 0)
                dve.tensor_copy(zt_hi[:, :, :, :], zt_f[:, :, :, :]).then_inc(zt_step, 1)
                need(dve, zt_step, b, 2, 2)
                dve.tensor_copy(zt[:, :, :, 0:4], zt_hi[:, :, :, :].bitcast(F32)).then_inc(zt_ready, 1)
                dve.tensor_tensor(zt[:, :, :, 4:8], zt_f[:, :, :, :], zt_hi[:, :, :, :].bitcast(F32),
                                  ALU.subtract).then_inc(zt_ready, 1)

            def gate_z(b, c):
                need(dve, zb_ready, b, NC, c + 1)
                need(dve, th_ready, b, NC, c + 1)
                need(dve, o_ready, b, NC, c - 1)
                dve.scalar_tensor_tensor(gz[:, c % 2, :], th[:, c, :], 1.0, zbank(b, c)[:, :],
                                         ALU.add, ALU.mult).then_inc(gz_ready, 1)

            def gate_numerator(b, c):
                need(dve, gz_ready, b, NC, c + 1)
                need(dve, num_ready, b, NC, c + 1)
                dve.tensor_tensor(o[:, c, :], gz[:, c % 2, :], numbank(b, c)[:, :],
                                  ALU.mult).then_inc(o_ready, 1)

            def moments_attn(b):
                need(dve, attn_tr, b, 1, 1)
                need(dve, n1_ready, b, NT, 0)
                moments(lambda t: sbank[:, P * t:P * t + P], stats1, mv1, st1, var1, b)

            def norm_attn(b):
                need(dve, rs1, b, 1, 1)
                need(dve, x1_ready, b, 1, 0)
                for t in range(NT):
                    dve.tensor_scalar(n1[:, t, :], sbank[:, P * t:P * t + P], mv1[:, t, 0:1], rstd1[:, t:t + 1],
                                      ALU.subtract, ALU.mult).then_inc(n1_ready, 1)

            def moments_x1(b):
                need(dve, x1_ready, b, 1, 1)
                need(dve, x2n_ready, b, NT, 0)
                moments(lambda t: x1[:, t, :], stats2, mv2, st2, var2, b)

            def offsets_x1(b):
                need(dve, rs2, b, 1, 1)
                dve.scalar_tensor_tensor(nmr2[:, :], mv2[:, :, 0], -1.0, rstd2[:, :],
                                         ALU.mult, ALU.mult).then_inc(nmr2_ready, 1)

            def shift_r(b):
                need(dve, dx_ready, b, 1, 1)
                need(dve, mr_ready, b, 1, 0)
                dve.scalar_tensor_tensor(xr, dx, mu[:, 0:1], x2t[:, 0:T],
                                         ALU.mult, ALU.add).then_inc(xr_ready, 1)

            def shift_k(b):
                need(dve, mk_ready, b, 1, 0)
                dve.scalar_tensor_tensor(xk, dx, mu[:, 1:2], x2t[:, 0:T],
                                         ALU.mult, ALU.add).then_inc(xk_ready, 1)

            def mix(b):
                need(dve, mv_ready, b, 1, 1)
                need(dve, rt_ready, b, 1, 1)
                need(dve, mix_tr, b, 1, 0)
                dve.scalar_tensor_tensor(mix_t[:, :], r_t, 1.0, sbank[:, :],
                                         ALU.add, ALU.mult).then_inc(mix_ready, 1)

            def moments_mix(b):
                need(dve, mix_tr, b, 1, 1)
                need(dve, n3_ready, b, NT, 0)
                moments(lambda t: sbank[:, P * t:P * t + P], stats3, mv3, st3, var3, b)

            def offsets_mix(b):
                need(dve, rs3, b, 1, 1)
                dve.scalar_tensor_tensor(nmr3[:, :], mv3[:, :, 0], -1.0, rstd3[:, :],
                                         ALU.mult, ALU.mult).then_inc(nmr3_ready, 1)

            def centre(dst, src, last_rows, s):
                dve.tensor_tensor(dst, src, last_rows, ALU.subtract).then_inc(s, 1)

            def rest_w(n, src, count):
                dve.wait_ge(w_hi_ready, count)
                dve.tensor_tensor(w_lo[n][:, :], src, w_hi[n][:, :].bitcast(F32), ALU.subtract).then_inc(w_lo_ready, 1)

            def outputs_and_k(b, main, one, two):
                first = isinstance(b, int) and b == 0
                for i in range(NK):
                    if one and i == 0:
                        gate_z(b - 1, 0)
                    if two and i == 0:
                        offsets_x1(b - 2)
                    if main and i == 0 and not first:
                        rest_xt(b)
                    if one and i == 0:
                        gate_numerator(b - 1, 0)
                        gate_z(b - 1, 1)
                        gate_numerator(b - 1, 1)
                    if one and i == 2:
                        gate_z(b - 1, 3)
                        gate_numerator(b - 1, 3)
                    if one and i > 3:
                        gate_z(b - 1, i)
                        gate_numerator(b - 1, i)
                    if two and i == NK - 1:
                        mix(b - 2)
                    if main:
                        elu_k(b, i)
                    if one and i == 0:
                        gate_z(b - 1, 2)
                        gate_numerator(b - 1, 2)
                    if two and i == 3:
                        shift_r(b - 2)
                    if two and i == 4:
                        shift_k(b - 2)
                    if first and i == 1:
                        dve.wait_ge(ld_w["q"], 64)
                        centre(w_f["q"], w_f["q"], w_last["q"], w_cent)
                    if first and i == 2:
                        rest_w("q", w_f["q"], 1)
                    if first and i == 3:
                        dve.wait_ge(ld_w["g"], 80)
                        centre(w_f["g"], w_f["g"], w_last["g"], w_cent)
                    if first and i == 4:
                        rest_w("g", w_f["g"], 2)
                    if first and i == 5:
                        dve.wait_ge(ld_cst, 16)
                        dve.tensor_copy(wv_aug[:, :, D:KVW],
                                        ones_row.rearrange("p (h w) -> p h w", w=2)).then_inc(wv_ready, 1)
                        dve.wait_ge(ld_w["v"], 64)
                        centre(wv_aug[:, :, 0:D], w_f["v"].rearrange("p (h d) -> p h d", d=D),
                               w_last["v"].rearrange("p (h d) -> p h d", d=D), wv_ready)
                    if first and i == 6:
                        rest_w("o", wo_f, 3)

            def q_and_gate(b, one, two, ahead):
                first = isinstance(b, int) and b == 0
                if ahead:
                    moments_x(b + 1)
                for c in range(NC):
                    elu_q(b, c)
                    if two and c == 0:
                        moments_mix(b - 2)
                    if c == 1:
                        take_ktx(b, 0)
                    if c == 2:
                        take_ktx(b, 1)
                    if two and c == 2:
                        offsets_mix(b - 2)
                    if ahead and c == 3:
                        norm_x(b + 1)
                    if c == 4:
                        take_ksum(b, 0)
                    if c == 5:
                        take_ksum(b, 1)
                if one:
                    moments_attn(b - 1)
                take_den(b)
                if one:
                    norm_attn(b - 1)
                reciprocals(b)
                if first:
                    dve.tensor_copy(sel[:, :, :], sel_f.rearrange("p (c n) -> p c n", n=P)).then_inc(sel_ready, 1)
                if one:
                    moments_x1(b - 1)

            dve.memset(minus1[:, :], -1.0)
            dve.memset(power[:, :], -0.5)
            dve.memset(x2t[:, 0:1], 0.0)
            dve.memset(xn[:, :, C - 1:C], 1.0).then_inc(fills, 1)
            dve.memset(kv[:, :, :], 0.0)
            dve.memset(zt[:, :, :, :], 0.0)
            moments_x(0)
            norm_x(0)
            dve.wait_ge(ld_fill, 32)
            dve.wait_ge(ld_w["k"], 64)
            for half in range(2):
                cols = slice(HALF * half, HALF * half + HALF)
                centre(w_f["k"][:, cols], w_f["k"][:, cols], w_last["k"][:, cols], w_cent)
            rest_xt(0)
            for half in range(2):
                cols = slice(HALF * half, HALF * half + HALF)
                dve.wait_ge(wk_hi_ready, half + 1)
                dve.tensor_tensor(w_lo["k"][:, cols], w_f["k"][:, cols], w_hi["k"][:, cols].bitcast(F32),
                                  ALU.subtract).then_inc(wk_lo_ready, 1)
            outputs_and_k(0, True, False, False)
            q_and_gate(0, False, False, True)
            outputs_and_k(1, True, True, False)
            q_and_gate(1, True, False, True)
            with dve.Fori(2, B - 1) as b:
                outputs_and_k(b, True, True, True)
                q_and_gate(b, True, True, True)
            outputs_and_k(B - 1, True, True, True)
            q_and_gate(B - 1, True, True, False)
            outputs_and_k(B, False, True, True)
            moments_mix(B - 2)
            offsets_mix(B - 2)

            for h in range(2):
                dve.wait_ge(last["attn_tr"], h + 1)
                moments(lambda t: bank[h][:, P * t:P * t + P], stats1, mv1, last["stats"], last["var"], h, tiles(h))
            dve.wait_ge(x1_ready, B - 1)
            dve.wait_ge(ld_res, 16 * B)
            for h in range(2):
                dve.wait_ge(last["rstd"], 1 + h)
                for t in range(NT)[tiles(h)]:
                    step = dve.tensor_scalar(n1[:, t, :], bank[h][:, P * t:P * t + P], mv1[:, t, 0:1],
                                             rstd1[:, t:t + 1], ALU.subtract, ALU.mult)
                step.then_inc(last["n1"], 1)
                dve.wait_ge(last["n1"], h + 1)
                dve.tensor_tensor(last_x1[:, tiles(h), :], n1[:, tiles(h), :], x_res[:, tiles(h), :],
                                  ALU.add).then_inc(last["x1"], 1)
            for h in range(2):
                dve.wait_ge(last["x1"], h + 1)
                moments(lambda t: last_x1[:, t, :], stats2, mv2, last["stats"], last["var"], 2 + h, tiles(h))
            dve.wait_ge(x2_tr, B - 1)
            for h in range(2):
                dve.wait_ge(last["rstd"], 3 + h)
                for t in range(NT)[tiles(h)]:
                    step = dve.tensor_scalar(x2n[:, t, :], last_x1[:, t, :], mv2[:, t, 0:1], rstd2[:, t:t + 1],
                                             ALU.subtract, ALU.mult)
                step.then_inc(last["x2n"], 1)
            dve.wait_ge(mk_ready, B - 1)
            for h in range(2):
                prev = x2t[:, tokens(h)]
                dve.wait_ge(last["x2t"], h + 1)
                dve.tensor_tensor(dx[:, tokens(h)], x2t[:, T // 2 * h + 1:T // 2 * (h + 1) + 1], prev,
                                  ALU.subtract).then_inc(last["dx"], 1)
                dve.wait_ge(last["dx"], h + 1)
                dve.scalar_tensor_tensor(xk[:, tokens(h)], dx[:, tokens(h)], mu[:, 1:2], prev,
                                         ALU.mult, ALU.add).then_inc(last["xk"], 1)
                dve.scalar_tensor_tensor(xr[:, tokens(h)], dx[:, tokens(h)], mu[:, 0:1], prev,
                                         ALU.mult, ALU.add).then_inc(last["xr"], 1)
            dve.wait_ge(mv_ready, B - 1)
            for h in range(2):
                dve.wait_ge(last["relu"], h + 1)
                dve.tensor_tensor(k_act[:, tokens(h)], k_relu[:, tokens(h)], bank[4 + h][:, tokens(h)],
                                  ALU.mult).then_inc(last["kact"], 1)
            dve.wait_ge(mix_tr, B - 1)
            for h in range(2):
                dve.wait_ge(last["mv"], h + 1)
                dve.wait_ge(last["r"], h + 1)
                dve.scalar_tensor_tensor(mix_t[:, tokens(h)], r_t[:, tokens(h)], 1.0, bank[h][:, tokens(h)],
                                         ALU.add, ALU.mult).then_inc(last["mix"], 1)
            for h in range(2):
                dve.wait_ge(last["mix_tr"], h + 1)
                moments(lambda t: bank[2 + h][:, P * t:P * t + P], stats3, mv3,
                        last["stats"], last["var"], 4 + h, tiles(h))
            dve.wait_ge(n3_ready, (B - 1) * NT)
            for h in range(2):
                dve.wait_ge(last["rstd"], 5 + h)
                dve.scalar_tensor_tensor(nmr3[:, tiles(h)], mv3[:, tiles(h), 0], -1.0, rstd3[:, tiles(h)],
                                         ALU.mult, ALU.mult).then_inc(last["offsets"], 1)
            dve.wait_ge(st_out, 16 * (B - 1))
            for h in range(2):
                dve.wait_ge(last["n3"], 2 * h + 2)
                dve.tensor_tensor(y_out[:, tiles(h), :], n3[:, tiles(h), :], last_x1[:, tiles(h), :],
                                  ALU.add).then_inc(last["y"], 1)

        @block.gpsimd
        def _(pool):
            def rsqrt(b, var_ready, mv, rstd, s):
                need(pool, var_ready, b, 1, 1)
                pool.tensor_tensor(rstd[:, :], mv[:, :, 1], power[:, :], ALU.pow).then_inc(s, 1)

            def split_x(b):
                need(pool, xnhi_ready, b, 1, 1)
                need(pool, k_used, b, NK, 0)
                pool.tensor_tensor(xn_lo[:, :, :], xn[:, :, :], xn_hi[:, :, :].bitcast(F32),
                                   ALU.subtract).then_inc(xnlo_ready, 1)

            def rest_k(b, i):
                need(pool, khi_ready, b, NK, i + 1)
                need(pool, k_used, b, NK, i + 1 - RING)
                pool.tensor_tensor(k_lo[:, i % RING, :], k[:, i, :],
                                   k_hi[:, i % RING, :].bitcast(F32), ALU.subtract).then_inc(klo_ready, 1)

            def rest_o(b, c):
                need(pool, ohi_ready, b, NC, c + 1)
                need(pool, o_used, b, NC, c + 1 - RING)
                pool.tensor_tensor(o_lo[:, c % RING, :], o[:, c, :],
                                   o_hi[:, c % RING, :].bitcast(F32), ALU.subtract).then_inc(olo_ready, 1)

            def residual1(b):
                need(pool, n1_ready, b, NT, NT)
                need(pool, ld_res, b, 16, 16)
                need(pool, y_ready, b, 1, 0)
                pool.tensor_tensor(x1[:, :, :], n1[:, :, :], x_res[:, :, :], ALU.add).then_inc(x1_ready, 1)

            def difference(b):
                need(pool, x2t_ready, b, 1, 1)
                need(pool, xk_ready, b, 1, 0)
                pool.tensor_tensor(dx, x2t[:, 1:T + 1], x2t[:, 0:T], ALU.subtract).then_inc(dx_ready, 1)

            def residual2(b):
                need(pool, n3_ready, b, NT, NT)
                need(pool, st_out, b, 16, 0)
                pool.tensor_tensor(y_out[:, :, :], n3[:, :, :], x1[:, :, :], ALU.add).then_inc(y_ready, 1)

            def outputs_and_k(b, main, one, two):
                for i in range(NK):
                    if main and i == 0:
                        split_x(b)
                    if two and i == 2:
                        difference(b - 2)
                    if one:
                        rest_o(b - 1, i)
                    if main:
                        rest_k(b, i)

            def q_and_gate(b, one, two, ahead):
                if ahead:
                    rsqrt(b + 1, var0, mv0, rstd0, rs0)
                if two:
                    rsqrt(b - 2, var3, mv3, rstd3, rs3)
                if two:
                    residual2(b - 2)
                if one:
                    rsqrt(b - 1, var1, mv1, rstd1, rs1)
                    residual1(b - 1)
                    rsqrt(b - 1, var2, mv2, rstd2, rs2)

            pool.wait_ge(fills, 1)
            rsqrt(0, var0, mv0, rstd0, rs0)
            outputs_and_k(0, True, False, False)
            q_and_gate(0, False, False, True)
            outputs_and_k(1, True, True, False)
            q_and_gate(1, True, False, True)
            with pool.Fori(2, B - 1) as b:
                outputs_and_k(b, True, True, True)
                q_and_gate(b, True, True, True)
            outputs_and_k(B - 1, True, True, True)
            q_and_gate(B - 1, True, True, False)
            outputs_and_k(B, False, True, True)
            rsqrt(B - 2, var3, mv3, rstd3, rs3)
            pool.wait_ge(n1_ready, (B - 1) * NT)
            pool.wait_ge(x2n_ready, (B - 1) * NT)
            for i, (mv, rstd) in enumerate(((mv1, rstd1), (mv2, rstd2), (mv3, rstd3))):
                for h in range(2):
                    pool.wait_ge(last["var"], 2 * i + h + 1)
                    pool.tensor_tensor(rstd[:, tiles(h)], mv[:, tiles(h), 1], power[:, tiles(h)],
                                       ALU.pow).then_inc(last["rstd"], 1)
                if i == 0:
                    residual2(B - 2)


_INS = ['L0_attn_x', 'L0_attn_Wq', 'L0_attn_Wk', 'L0_attn_Wv', 'L0_attn_Wg', 'L0_attn_bg', 'L0_attn_Wo',
        'L0_ffn_W_r', 'L0_ffn_W_k', 'L0_ffn_W_v', 'L0_ffn_mu_r', 'L0_ffn_mu_k']


def kernel(**inputs):
    import concourse.bacc as _bacc
    from concourse.bass_utils import run_bass_kernel_spmd as _run

    nc = _bacc.Bacc("TRN2", target_bir_lowering=False, num_devices=1)
    arrays = {f"in_{n}_dram": np.ascontiguousarray(inputs[n]) for n in _INS}
    arrays["in_consts_dram"] = constants()
    arrays["in_fill_dram"] = row_fill()
    args = [nc.dram_tensor(n, a.shape, mybir.dt.from_np(a.dtype), kind="ExternalInput").ap()
            for n, a in arrays.items()]
    args.append(nc.dram_tensor("out_0_dram", (B, T, C), F32, kind="ExternalOutput").ap())
    sandwich(nc, *args)
    r = _run(nc, [arrays], core_ids=[0])
    return r.results[0]["out_0_dram"]
```
